# Optimizing a Trainium2 kernel written in Bass

```python
import numpy as np
import jax
import jax.numpy as jnp

def _softmax(x, axis=-1):
    return jax.nn.softmax(x, axis=axis)

def _gelu(x):
    return jax.nn.gelu(x, approximate=True)

def _silu(x):
    return jax.nn.silu(x)

def _sigmoid(x):
    return jax.nn.sigmoid(x)

def _layernorm(x, axis=-1, eps=1e-05):
    m = jnp.mean(x, axis=axis, keepdims=True)
    v = jnp.var(x, axis=axis, keepdims=True)
    return (x - m) / jnp.sqrt(v + eps)

def _scatter_add(tgt, idx, src, axis=0):
    return tgt.at[idx].add(src)

def _segment_sum(src, seg, n):
    return jax.ops.segment_sum(src, seg, n)
kernel_name = 'mk_gps_d1_gnn_r8_8a821f'

def setup_inputs(seed: int=0):
    np.random.seed(seed)
    _w = jnp.asarray

    def _rec_inputs():
        import jax
        import jax.numpy as jnp
        _gk = jax.random.key(seed)
        x = -0.0003713 + 1 * jax.random.normal(jax.random.fold_in(_gk, 1), (6250, 256), jnp.float32)
        src = jax.random.randint(jax.random.fold_in(_gk, 2), (100000,), 0, 6250, jnp.int32)
        dst = jax.random.randint(jax.random.fold_in(_gk, 3), (100000,), 0, 6250, jnp.int32)
        _o = jnp.argsort(dst, stable=True)
        src = src[_o]
        dst = dst[_o]
        edge_type_16 = jax.random.randint(jax.random.fold_in(_gk, 12), (100000,), 0, 16, jnp.int32)
        edge_weight1 = jax.random.uniform(jax.random.fold_in(_gk, 13), (100000, 1), jnp.float32, 0.0, 1)
        return (x, src, dst, edge_type_16, edge_weight1)
    x, src, dst, edge_type_16, edge_weight1 = _rec_inputs()

    def _L0_gnn_setup():
        import jax, jax.numpy as jnp
        import numpy as np
        N_NODES = 6250
        N_EDGES = 100000
        NUM_RELS = 16
        FEAT = 256
        OUT = 256
        key = jax.random.key(seed)
        ks = jax.random.split(key, 7)
        h = jax.random.normal(ks[0], (N_NODES, FEAT), dtype=jnp.float32)
        norm = jax.random.uniform(ks[1], (N_EDGES, 1), dtype=jnp.float32)
        weight = jax.random.normal(ks[2], (NUM_RELS, FEAT, OUT), dtype=jnp.float32) * 0.05
        gate_weight = jax.random.normal(ks[3], (NUM_RELS, FEAT, 1), dtype=jnp.float32) * 0.05
        src = jax.random.randint(ks[4], (N_EDGES,), 0, N_NODES)
        dst = jax.random.randint(ks[5], (N_EDGES,), 0, N_NODES)
        rel_type = jax.random.randint(ks[6], (N_EDGES,), 0, NUM_RELS)
        return {'h': h, 'norm': norm, 'weight': weight, 'gate_weight': gate_weight, 'src': src, 'dst': dst, 'rel_type': rel_type}
    _L0_gnn_all = _L0_gnn_setup()
    _L0_gnn_in = {k: v for k, v in _L0_gnn_all.items() if k in ('weight', 'gate_weight')}
    del _L0_gnn_all

    def _L0_mix_setup():
        import jax, jax.numpy as jnp
        import numpy as np
        HEADS = 8
        DIM_HEAD = 64
        EPS = 1e-05

        def _inst_norm(t):
            mu = jnp.mean(t, axis=-1, keepdims=True)
            var = jnp.var(t, axis=-1, keepdims=True)
            return (t - mu) / jnp.sqrt(var + EPS)
        key = jax.random.key(seed)
        k1, k2, k3, k4 = jax.random.split(key, 4)
        b, n, dim = (4, 1024, 256)
        inner = HEADS * DIM_HEAD
        x = jax.random.normal(k1, (b, n, dim), dtype=jnp.float32)
        w_qkv = jax.random.normal(k2, (dim, 3 * inner), dtype=jnp.float32) * (1.0 / DIM_HEAD)
        w_out = jax.random.normal(k3, (inner, dim), dtype=jnp.float32) * dim ** (-0.5)
        b_out = jax.random.normal(k4, (dim,), dtype=jnp.float32) * 0.01
        return {'x': x, 'w_qkv': w_qkv, 'w_out': w_out, 'b_out': b_out}
    _L0_mix_all = _L0_mix_setup()
    _L0_mix_in = {k: v for k, v in _L0_mix_all.items() if k in ('w_qkv', 'w_out', 'b_out')}
    del _L0_mix_all

    def _L0_ffn_setup():
        import jax, jax.numpy as jnp
        import numpy as np
        NUM_EXPERTS = 8
        TOP_K = 2
        B, S, D = (8, 1024, 256)

        def _moe(tokens, router_w, w1, b1, w2, b2):
            N = tokens.shape[0]
            E = router_w.shape[0]
            logits = tokens.astype(jnp.float32) @ router_w.astype(jnp.float32).T
            probs = jax.nn.softmax(logits, axis=-1)
            rw, re = jax.lax.top_k(probs, TOP_K)
            if TOP_K > 1:
                rw = rw / jnp.maximum(rw.sum(-1, keepdims=True), 1e-12)
            rw = rw.astype(tokens.dtype)
            combine = jnp.zeros((N, E), tokens.dtype).at[jnp.arange(N)[:, None], re].set(rw)
            out = tokens
            for e in range(E):
                h = jax.nn.gelu(tokens @ w1[e] + b1[e], approximate=False)
                y = h @ w2[e] + b2[e]
                out = out + combine[:, e:e + 1] * y
            return out
        key = jax.random.key(seed)
        ks = jax.random.split(key, 4)
        scale = 1.0 / np.sqrt(D).astype(np.float32)
        return {'input_embeddings': jax.random.normal(ks[0], (B, S, D), jnp.float32), 'router_w': jax.random.normal(ks[1], (NUM_EXPERTS, D), jnp.float32) * scale, 'w1': jax.random.normal(ks[2], (NUM_EXPERTS, D, D), jnp.float32) * scale, 'b1': jnp.zeros((NUM_EXPERTS, D), jnp.float32), 'w2': jax.random.normal(ks[3], (NUM_EXPERTS, D, D), jnp.float32) * scale, 'b2': jnp.zeros((NUM_EXPERTS, D), jnp.float32)}
    _L0_ffn_all = _L0_ffn_setup()
    _L0_ffn_in = {k: v for k, v in _L0_ffn_all.items() if k in ('router_w', 'w1', 'b1', 'w2', 'b2')}
    del _L0_ffn_all
    return {'x': x, 'src': src, 'dst': dst, 'edge_type_16': edge_type_16, 'edge_weight1': edge_weight1, 'L0_gnn_weight': _L0_gnn_in['weight'], 'L0_gnn_gate_weight': _L0_gnn_in['gate_weight'], 'L0_mix_w_qkv': _L0_mix_in['w_qkv'], 'L0_mix_w_out': _L0_mix_in['w_out'], 'L0_mix_b_out': _L0_mix_in['b_out'], 'L0_ffn_router_w': _L0_ffn_in['router_w'], 'L0_ffn_w1': _L0_ffn_in['w1'], 'L0_ffn_b1': _L0_ffn_in['b1'], 'L0_ffn_w2': _L0_ffn_in['w2'], 'L0_ffn_b2': _L0_ffn_in['b2']}

def reference(x, src, dst, edge_type_16, edge_weight1, L0_gnn_weight, L0_gnn_gate_weight, L0_mix_w_qkv, L0_mix_w_out, L0_mix_b_out, L0_ffn_router_w, L0_ffn_w1, L0_ffn_b1, L0_ffn_w2, L0_ffn_b2):
    import jax
    import jax.numpy as jnp

    def _L0_gnn_ref(h, norm, weight, gate_weight, src, dst, rel_type):
        import jax, jax.numpy as jnp
        import numpy as np
        N_NODES = 6250
        N_EDGES = 100000
        NUM_RELS = 16
        FEAT = 256
        OUT = 256
        n_nodes = h.shape[0]
        all_msg = jnp.einsum('nf,rfo->rno', h, weight)
        msg = all_msg[rel_type, src] * norm
        all_gate = jnp.einsum('nf,rf->rn', h, gate_weight[..., 0])
        gate = jax.nn.sigmoid(all_gate[rel_type, src])[:, None]
        msg = msg * gate
        agg = jax.ops.segment_sum(msg, dst, num_segments=n_nodes)
        return jax.nn.relu(agg)

    def _L0_mix_ref(x, w_qkv, w_out, b_out):
        import jax, jax.numpy as jnp
        import numpy as np
        HEADS = 8
        DIM_HEAD = 64
        EPS = 1e-05

        def _inst_norm(t):
            mu = jnp.mean(t, axis=-1, keepdims=True)
            var = jnp.var(t, axis=-1, keepdims=True)
            return (t - mu) / jnp.sqrt(var + EPS)
        b, n, dim = x.shape
        qkv = x @ w_qkv
        q, k, v = jnp.split(qkv, 3, axis=-1)
        to_heads = lambda t: t.reshape(b, n, HEADS, DIM_HEAD).transpose(0, 2, 1, 3)
        q, k, v = (to_heads(q), to_heads(k), to_heads(v))
        k = _inst_norm(k)
        v = _inst_norm(v)
        dots = jnp.einsum('bhnd,bhne->bhde', k, v)
        out = jnp.einsum('bhnd,bhde->bhne', q, dots) * (1.0 / n)
        out = out.transpose(0, 2, 1, 3).reshape(b, n, HEADS * DIM_HEAD)
        return out @ w_out + b_out

    def _L0_ffn_ref(input_embeddings, router_w, w1, b1, w2, b2):
        import jax, jax.numpy as jnp
        import numpy as np
        NUM_EXPERTS = 8
        TOP_K = 2
        B, S, D = (8, 1024, 256)

        def _moe(tokens, router_w, w1, b1, w2, b2):
            N = tokens.shape[0]
            E = router_w.shape[0]
            logits = tokens.astype(jnp.float32) @ router_w.astype(jnp.float32).T
            probs = jax.nn.softmax(logits, axis=-1)
            rw, re = jax.lax.top_k(probs, TOP_K)
            if TOP_K > 1:
                rw = rw / jnp.maximum(rw.sum(-1, keepdims=True), 1e-12)
            rw = rw.astype(tokens.dtype)
            combine = jnp.zeros((N, E), tokens.dtype).at[jnp.arange(N)[:, None], re].set(rw)
            out = tokens
            for e in range(E):
                h = jax.nn.gelu(tokens @ w1[e] + b1[e], approximate=False)
                y = h @ w2[e] + b2[e]
                out = out + combine[:, e:e + 1] * y
            return out
        b, s, d = input_embeddings.shape
        tokens = input_embeddings.reshape(b * s, d)
        return _moe(tokens, router_w, w1, b1, w2, b2).reshape(b, s, d)
    xn = _layernorm(x, axis=-1)
    x = x + _L0_gnn_ref(xn, edge_weight1, L0_gnn_weight, L0_gnn_gate_weight, src, dst, edge_type_16) + _L0_mix_ref(xn[None], L0_mix_w_qkv, L0_mix_w_out, L0_mix_b_out)[0]
    x = x + _L0_ffn_ref(_layernorm(x, axis=-1)[None], L0_ffn_router_w, L0_ffn_w1, L0_ffn_b1, L0_ffn_w2, L0_ffn_b2)[0]
    return x

_drawn_inputs = setup_inputs


def setup_inputs(seed=0):
    import zlib

    import numpy as np

    out = dict(_drawn_inputs(seed))
    spreads = {'L0_ffn_b1': (0.0, 0.355), 'L0_ffn_b2': (0.0, 0.1)}
    factors = {'L0_mix_b_out': 3.867}
    for name, (base, spread) in spreads.items():
        noise = np.random.default_rng([zlib.crc32(name.encode()), seed]).standard_normal(out[name].shape)
        drawn = base * np.exp(spread * noise) if base else spread * noise
        out[name] = jnp.asarray(drawn.astype(out[name].dtype))
    for name, factor in factors.items():
        out[name] = (out[name] * factor).astype(out[name].dtype)
    return out
```

```python
from contextlib import ExitStack

import concourse.bass as bass
from concourse import mybir

F32 = mybir.dt.float32
I32 = mybir.dt.int32
U32 = mybir.dt.uint32
ALU = mybir.AluOpType
ACT = mybir.ActivationFunctionType
AX = mybir.AxisListType

P = 128
EPS = 1e-5
BANK = 512
CHUNKS = 4
BATCH = CHUNKS * P
WINDOW = P
GROUP = 4
LAG = 3
BASES = 4


class Streams:

    def __init__(self, nc, ctx):
        self.nc, self.ctx = nc, ctx
        self.queue = {e: [] for e in ("sync", "scalar", "vector", "gpsimd", "tensor")}
        self.sems, self.value, self.seen = {}, {}, {}

    def sem(self, name):
        if name not in self.sems:
            self.sems[name] = self.ctx.enter_context(self.nc.semaphore("s_" + name))
            self.value[name] = 0
        return self.sems[name]

    def put(self, engine, step, make, after=(), by=1):
        waits = []
        for name, value in after:
            if self.seen.get((engine, name), 0) < value:
                self.seen[engine, name] = value
                waits.append((self.sem(name), value))
        sem = self.sem(step) if step else None

        def emit(eng):
            for s, value in waits:
                eng.wait_ge(s, value)
            made = make(eng)
            if sem is not None:
                made.then_inc(sem, by)

        self.queue[engine].append(emit)
        if not step:
            return None
        self.value[step] += by
        return step, self.value[step]

    def dma(self, step, out, in_, after=(), engine="sync"):
        return self.put(engine, step, lambda e: e.dma_start(out, in_), after, by=16)


def gps_layer(nc, x, src, dst, rel, norm, w_rel, w_gate, w_qkv, w_out, b_out, w_router, w1, b1, w2, b2, out):
    N, D = x.shape
    E = src.shape[0]
    R = w_rel.shape[0]
    X = w1.shape[0]
    INNER = w_out.shape[0]
    HEAD = 64
    KH = D // P
    PAIRS = INNER // P
    VK = 2 * INNER
    TILES = -(-N // P)
    LAST = N - (TILES - 1) * P
    GROUPS = -(-TILES // GROUP)
    BATCHES = -(-E // BATCH)
    TAIL = E - (BATCHES - 1) * BATCH
    BLOCK = (BATCHES - 97, 97)
    FIRST = (0, BLOCK[0])
    assert D == 2 * P and D % P == 0 and BLOCK[0] <= P and E % BATCH and R * D % BANK == 0
    NB = R * D // BANK
    PER = BANK // D
    AGG = TILES * P + WINDOW

    ctx = ExitStack()
    with ctx:
        S = Streams(nc, ctx)

        def sb(name, shape, dt=F32):
            return ctx.enter_context(nc.sbuf_tensor(name, shape, dt))

        bank = [ctx.enter_context(nc.psum_tensor(f"bank{i}", [P, BANK], F32)) for i in range(8)]
        table = nc.dram_tensor("messages", [N, R * D], F32, kind="Internal").ap()
        xnT_dram = nc.dram_tensor("xnT_scratch", [GROUPS, P, KH, GROUP * P], F32, kind="Internal").ap()

        ident = sb("ident", [P, P])
        iota_i = sb("iota_i", [P, P], I32)
        iota = sb("iota", [P, P])
        w1_s = sb("w1_s", [P, KH, X, D])
        w2_s = sb("w2_s", [P, KH, X, D])
        b2_s = sb("b2_s", [X, D])
        small = sb("small", [P, 96])
        gateT, routerT = small[:, 0:2 * R], small[:, 2 * R:2 * R + 2 * X]
        boutT = small[:, 2 * R + 2 * X:2 * R + 2 * X + KH]
        b1T = small[:, 64:64 + KH * X]
        idxT = sb("idxT", [P, CHUNKS, BATCHES], I32)
        dstT = sb("dstT", [P, CHUNKS, BATCHES])
        offT = sb("offT", [P, CHUNKS, BATCHES])
        nrmT = sb("nrmT", [P, CHUNKS, BATCHES])
        rows = sb("rows", [1, 6, BATCHES])
        basei = sb("basei", [1, BATCHES], I32)
        carrier = sb("carrier", [P, 1], I32)
        slowi = sb("slowi", [1, 1], I32)
        flag = sb("flag", [1, 8])
        slow_all = sb("slow_all", [P, 1])
        ones1 = sb("ones1", [1, P])
        mix = sb("mix", [P, KH, D])
        agg = sb("agg", [P, KH, AGG])

        ARENA = 23 * 1024 + 256
        arena = sb("arena", [P, ARENA])
        top = [0]

        def carve(*shape):
            n = 1
            for s in shape:
                n *= s
            v = arena[:, top[0]:top[0] + n]
            top[0] += n
            assert top[0] <= ARENA
            names = " ".join("abcd"[:len(shape)])
            return v.rearrange(f"p ({names}) -> p {names}", **dict(zip("abcd", shape))) if len(shape) > 1 else v

        w_s = carve(KH, R * D)
        wkv_s = carve(KH, VK)
        x_ring = carve(4, D)
        xn_ring = carve(2, D)
        xnT_ring = carve(3, KH, P)
        gate_ring = carve(2, R)
        sq = carve(VK)
        v_s = carve(INNER)
        k_s = carve(INNER)
        stA = carve(2, 16)
        mvA = carve(2, 4)
        hs = carve(6, 2 * INNER // HEAD)
        stage_at = top[0]
        stage = carve(2, R, D)
        top[0] = stage_at
        lists_f = [carve(2, BATCH) for _ in range(4)]
        idx_f, dst_f, off_f, nrm_f = lists_f
        ext = carve(2, 2)
        wq_s = carve(KH, INNER)
        lists_i = [carve(2, BATCH).bitcast(I32) for _ in range(3)]
        src_i, dst_i, rel_i = lists_i
        top[0] = stage_at
        bd = carve(PAIRS, P)
        fold = carve(PAIRS, D)
        LENT = 2 * PAIRS * D
        wqT, wout_s = (agg[:, KH - 1, AGG - LENT + i * PAIRS * D:AGG - LENT + (i + 1) * PAIRS * D].rearrange(
            "p (j o) -> p j o", j=PAIRS) for i in range(2))
        SLOTS = 6
        top[0] = 0
        msg = carve(SLOTS, CHUNKS, D)
        onehot = carve(2, CHUNKS, WINDOW)
        x_g = carve(2, GROUP, D)
        xnT_g = carve(2, KH, GROUP * P)
        acc = carve(2, GROUP, D)
        x3 = carve(GROUP, D)
        x3T = carve(2, KH, GROUP * P)
        h_s = carve(2, KH, GROUP * P)
        relu = carve(2, KH, P)
        stB = carve(GROUP, 8)
        mvB = carve(GROUP, 2)
        sdB = carve(4, GROUP)
        lgB = carve(3, GROUP, X)
        topB = carve(GROUP, 8)
        smB = carve(8, GROUP)
        wB = carve(2, GROUP, 2)
        combB = carve(2, GROUP, X)
        c2B = carve(2, GROUP, X)
        topi = sb("topi", [P, GROUP, 8], U32)
        combT = carve(GROUP * P)
        dstG, nrmG, idxG = carve(CHUNKS), carve(CHUNKS), sb("idxG", [P, CHUNKS], I32)

        V = lambda step, make, after=(): S.put("vector", step, make, after)
        A = lambda step, make, after=(): S.put("scalar", step, make, after)
        T = lambda step, make, after=(): S.put("tensor", step, make, after)
        G = lambda step, make, after=(): S.put("gpsimd", step, make, after)

        gate_rows, router_rows = sb("gate_rows", [R, D]), sb("router_rows", [X, D])
        bout_rows, b1_rows = sb("bout_rows", [KH, P]), sb("b1_rows", [KH * X, P])

        def tile_rows(t):
            return P if t < TILES - 1 else LAST

        x_loaded = {}

        def load_x(t):
            after = [xn_made[t - 4]] if t >= 4 else []
            if tile_rows(t) < P:
                z = V("x_pad", lambda e: e.memset(x_ring[:, t % 4, :], 0.0), after)
                after = after + [z]
            n = tile_rows(t)
            x_loaded[t] = S.dma(f"x_load{t % 4}", x_ring[0:n, t % 4, :], x[t * P:t * P + n, :], after)

        xn_made = {}
        for t in range(3):
            load_x(t)
        rows_in = [S.dma("rows_in", o, i) for o, i in (
            (gate_rows[:, :], w_gate.rearrange("r f a -> r (f a)")),
            (router_rows[:, :], w_router),
            (bout_rows[:, :], b_out.rearrange("(h p) -> h p", p=P)),
            (b1_rows[:, :], b1.rearrange("x (h p) -> (x h) p", p=P)))][-1]
        wkv_in = S.dma("wkv_in", wkv_s, w_qkv[:, INNER:].rearrange("(k p) c -> p k c", p=P))
        edges_in = []
        for a, t in zip((src, dst, rel, norm.rearrange("e a -> (e a)")), (src_i, dst_i, rel_i, nrm_f)):
            n0, n1 = BLOCK[0] * BATCH, (BATCHES - 1) * BATCH
            for o, i in ((t[0:BLOCK[0], 0, :], a[0:n0].rearrange("(b e) -> b e", e=BATCH)),
                         (t[0:BLOCK[1] - 1, 1, :], a[n0:n1].rearrange("(b e) -> b e", e=BATCH)),
                         (t[BLOCK[1] - 1:BLOCK[1], 1, 0:TAIL], a[n1:E].rearrange("(b e) -> b e", b=1))):
                edges_in.append(S.dma("edges_in", o, i, engine="scalar"))
        edges_in = edges_in[-1]
        wq_in = S.dma("wq_in", wq_s, w_qkv[:, 0:INNER].rearrange("(k p) c -> p k c", p=P))
        w_in = [S.dma(f"w_in{k}", w_s[:, k, :].rearrange("p (r o) -> p r o", r=R),
                      w_rel[:, k * P:(k + 1) * P, :].rearrange("r p o -> p r o")) for k in range(KH)]
        wout_in = S.dma("wout_in", wout_s, w_out.rearrange("(j p) o -> p j o", p=P))
        late = []
        for k in range(KH):
            late.append((w1_s[:, k, :, :], w1[:, k * P:(k + 1) * P, :].rearrange("x p o -> p x o")))
            late.append((w2_s[:, k, :, :], w2[:, k * P:(k + 1) * P, :].rearrange("x p o -> p x o")))
        late.append((b2_s[:, :], b2))
        for o, i in late:
            experts_in = S.dma("experts_in", o, i)

        z = G("pool_const", lambda e: e.memset(ident[:, :], 0.0))
        z = G("pool_const", lambda e: e.affine_select(
            out=ident[:, :], in_=ident[:, :], compare_op=ALU.not_equal, fill=1.0, base=0,
            pattern=[[-1, P]], channel_multiplier=1), [z])
        z = G("pool_const", lambda e: e.iota(iota_i[:, :], pattern=[[1, P]], base=0, channel_multiplier=0), [z])
        z = G("pool_const", lambda e: e.tensor_copy(iota[:, :], iota_i[:, :]), [z])
        z = G("pool_const", lambda e: e.memset(carrier[:, :], 0), [z])
        consts = G("pool_const", lambda e: e.memset(ones1[:, :], 1.0), [z])
        agg_zero = [G("agg_zero", lambda e, h=h: e.memset(agg[:, h, 0:AGG - LENT * (h == KH - 1)], 0.0))
                    for h in range(KH)]

        def turn_small(e):
            for h in range(KH):
                e.transpose(bank[7][:, h * R:(h + 1) * R], gate_rows[:, h * P:(h + 1) * P], ident[0:R, 0:R])
                e.transpose(bank[7][:, 2 * R + h * X:2 * R + (h + 1) * X], router_rows[:, h * P:(h + 1) * P],
                            ident[0:X, 0:X])
            e.transpose(bank[7][:, 2 * R + 2 * X:2 * R + 2 * X + KH], bout_rows[:, :], ident[0:KH, 0:KH])
            return e.transpose(bank[7][:, 64:64 + KH * X], b1_rows[:, :], ident[0:KH * X, 0:KH * X])

        t_small = T("turn_small", turn_small, [consts, rows_in])
        small_in = V("small_copy", lambda e: e.tensor_copy(small[:, 0:2 * R + 2 * X + KH],
                                                           bank[7][:, 0:2 * R + 2 * X + KH]), [t_small])
        small_in = V("small_copy", lambda e: e.tensor_copy(b1T, bank[7][:, 64:64 + KH * X]), [t_small])

        heads = VK // HEAD
        wmean = sq[:, 0:KH * heads]
        wkv_h = wkv_s.rearrange("p k (h d) -> p (k h) d", d=HEAD)
        c = V("center", lambda e: e.tensor_reduce(wmean, wkv_h, AX.X, ALU.add), [wkv_in])
        c = V("center", lambda e: e.tensor_scalar(wmean, wmean, 1.0 / HEAD, None, ALU.mult), [c])
        centered = V("center", lambda e: e.tensor_tensor(
            wkv_h, wkv_h, wmean.unsqueeze(2).to_broadcast([P, KH * heads, HEAD]), ALU.subtract), [c])

        slot = lambda t, n: t % n
        ln_var, ln_sd = {}, {}

        def ln_stats(t):
            i = slot(t, 2)
            s = V("ln_stats", lambda e: e.bn_stats(stA[:, i, 0:6], x_ring[:, t % 4, :]), [x_loaded[t]])
            s = V("ln_stats", lambda e: e.bn_aggr(mvA[:, i, 0:2], stA[:, i, 0:6]), [s])
            ln_var[t] = V("ln_stats", lambda e: e.tensor_scalar(mvA[:, i, 2:3], mvA[:, i, 1:2], EPS, None, ALU.add), [s])

        def ln_sqrt(t):
            i = slot(t, 2)
            ln_sd[t] = A("ln_sqrt", lambda e: e.activation(mvA[:, i, 3:4], mvA[:, i, 2:3], ACT.Sqrt), [ln_var[t]])

        turned, xnT_made, xnT_stored, gates_done, gate_made = {}, {}, {}, {}, {}
        table_read, kv_read, stored, evacuated = {}, {}, {}, []

        def normalize(t):
            i = slot(t, 2)
            r = V("ln_rstd", lambda e: e.reciprocal(mvA[:, i, 3:4], mvA[:, i, 3:4]), [ln_sd[t]])
            xn_made[t] = V("xn", lambda e: e.tensor_scalar(
                xn_ring[:, i, :], x_ring[:, t % 4, :], mvA[:, i, 0:1], mvA[:, i, 3:4], ALU.subtract, ALU.mult),
                [r] + ([turned[t - 2]] if t >= 2 else []))

        def turn(t):
            def make(e):
                for h in range(KH):
                    m = e.transpose(bank[6][:, h * P:(h + 1) * P], xn_ring[:, t % 2, h * P:(h + 1) * P], ident[:, :])
                return m
            turned[t] = T("turn_xn", make, [xn_made[t], consts] + ([xnT_made[t - 1]] if t else []))

        def copy_turned(t):
            after = [turned[t]] + ([table_read[t - 3], xnT_stored[t - 3]] if t >= 3 else [])
            xnT_made[t] = A("xnT", lambda e: e.copy(xnT_ring[:, t % 3, :, :],
                                                    bank[6][:, 0:D].rearrange("p (h n) -> p h n", h=KH)), after)
            g, k = divmod(t, GROUP)
            xnT_stored[t] = S.dma(f"xnT_store{t % 3}", xnT_dram[g, :, :, k * P:(k + 1) * P],
                                  xnT_ring[:, t % 3, :, :], [xnT_made[t]])

        def gates(t):
            def make(e):
                for h in range(KH):
                    m = e.matmul(bank[7][:, 0:R], xnT_ring[:, t % 3, h, :], gateT[:, h * R:(h + 1) * R],
                                 start=h == 0, stop=h == KH - 1)
                return m
            gates_done[t] = T("gates", make, [xnT_made[t], small_in] + ([gate_made[t - 1]] if t else []))

        def sigmoid(t):
            after = [gates_done[t]] + (evacuated[(t - 1) * NB - 2:(t - 1) * NB] if t >= 2 else [])
            gate_made[t] = A("gate", lambda e: e.activation(gate_ring[:, t % 2, :], bank[7][:, 0:R], ACT.Sigmoid), after)

        kv_done, dots_done, table_bank = {}, {}, {}

        def keys_values(t):
            def make(e):
                for c in range(VK // BANK):
                    for h in range(KH):
                        m = e.matmul(bank[3 + c][:, :], xnT_ring[:, t % 3, h, :], wkv_s[:, h, c * BANK:(c + 1) * BANK],
                                     start=h == 0, stop=h == KH - 1)
                return m
            kv_done[t] = T("keys_values", make, [xnT_made[t], centered] + (kv_read[t - 1] if t else []))

        squared, v_made, k_made, roots = {}, {}, {}, {}

        def head_squares(t):
            after = [kv_done[t]] + ([roots[t - 1]] if t else [centered])
            for c in range(2):
                squared[t] = A("squares", lambda e, c=c: e.activation(
                    sq[:, c * INNER:(c + 1) * INNER], bank[3 + c][:, :], ACT.Square), after)
            v_made[t] = A("values", lambda e: e.copy(v_s, bank[4][:, :]), [dots_done[t - 1]] if t else [])

        def head_vars(t):
            s = V("head_vars", lambda e: e.tensor_reduce(hs[:, 0, :], sq.rearrange("p (h d) -> p h d", d=HEAD),
                                                         AX.X, ALU.add), [squared[t]])
            s = V("head_vars", lambda e: e.tensor_scalar(hs[:, 1, :], hs[:, 0, :], 1.0 / HEAD, EPS, ALU.mult, ALU.add), [s])
            H = INNER // HEAD
            roots[t] = V("head_vars", lambda e: e.tensor_tensor(hs[:, 2, 0:H], hs[:, 1, 0:H], hs[:, 1, H:2 * H], ALU.mult), [s])

        def head_scale(t):
            H = INNER // HEAD
            q = A("head_sqrt", lambda e: e.activation(hs[:, 3, 0:H], hs[:, 2, 0:H], ACT.Sqrt), [roots[t]])
            r = V("keys", lambda e: e.reciprocal(hs[:, 4, 0:H], hs[:, 3, 0:H]), [q])
            k_made[t] = V("keys", lambda e: e.tensor_tensor(
                k_s.rearrange("p (h d) -> p h d", d=HEAD), bank[3][:, :].rearrange("p (h d) -> p h d", d=HEAD),
                hs[:, 4, 0:H].unsqueeze(2).to_broadcast([P, H, HEAD]), ALU.mult),
                [r] + ([dots_done[t - 1]] if t else []))
            kv_read[t] = [squared[t], v_made[t], k_made[t]]

        def dots(t):
            def make(e):
                for j in range(PAIRS):
                    m = e.matmul(bank[5][:, j * P:(j + 1) * P], v_s[:, j * P:(j + 1) * P], k_s[:, j * P:(j + 1) * P],
                                 start=t == 0 and j == 0, stop=t == TILES - 1, skip_group_check=True)
                return m
            dots_done[t] = T("dots", make, [v_made[t], k_made[t]])

        def messages(t, n):
            i = t * NB + n
            def make(e):
                for h in range(KH):
                    m = e.matmul(bank[i % 3][:, :], xnT_ring[:, t % 3, h, :], w_s[:, h, n * BANK:(n + 1) * BANK],
                                 start=h == 0, stop=h == KH - 1)
                return m
            table_bank[i] = T("messages", make, [xnT_made[t]] + w_in + ([evacuated[i - 3]] if i >= 3 else []))
            table_read[t] = table_bank[i]

        def evacuate(t, n):
            i = t * NB + n
            after = [table_bank[i], gate_made[t]] + ([stored[t - 2]] if t >= 2 else [edge_lists_done])
            for r in range(PER):
                o = stage[:, t % 2, n * PER + r, :]
                s = bank[i % 3][:, r * D:(r + 1) * D]
                g = gate_ring[:, t % 2, n * PER + r:n * PER + r + 1]
                if n % 2:
                    done = A("stage_act", lambda e, o=o, s=s, g=g: e.activation(o, s, ACT.Copy, scale=g), after)
                else:
                    done = V("stage_dve", lambda e, o=o, s=s, g=g: e.tensor_scalar(o, s, g, None, ALU.mult), after)
            evacuated.append(done)

        def store(t):
            n = tile_rows(t)
            stored[t] = S.dma(f"table_store{t % 2}", table[t * P:t * P + n, :],
                              stage[0:n, t % 2, :, :].rearrange("p r o -> p (r o)"), evacuated[-2:])

        for t in range(2):
            ln_stats(t)
            ln_sqrt(t)
            normalize(t)
        turn(0)
        copy_turned(0)
        gates(0)
        sigmoid(0)

        last = BLOCK[1] - 1
        p = []
        for t in (src_i, dst_i, rel_i):
            p.append(V("edge_pad", lambda e, t=t: e.tensor_copy(
                t[last:last + 1, 1, TAIL:BATCH], t[last:last + 1, 1, TAIL - 1:TAIL].to_broadcast([1, BATCH - TAIL])), [edges_in]))
        p.append(V("edge_pad", lambda e: e.memset(nrm_f[last:last + 1, 1, TAIL:BATCH], 0.0), [edges_in]))
        padded = p[-1]
        for k, n in enumerate(BLOCK):
            V("edge_idx", lambda e, k=k, n=n: e.scalar_tensor_tensor(
                idx_f[0:n, k, :], src_i[0:n, k, :], float(R), rel_i[0:n, k, :], ALU.mult, ALU.add), [padded])
            V("edge_dst", lambda e, k=k, n=n: e.tensor_copy(dst_f[0:n, k, :], dst_i[0:n, k, :]), [padded])
            lo = V("edge_ext", lambda e, k=k, n=n: e.tensor_reduce(ext[0:n, k, 0:1], dst_i[0:n, k, :], AX.X, ALU.min), [padded])
            V("edge_ext", lambda e, k=k, n=n: e.tensor_reduce(ext[0:n, k, 1:2], dst_i[0:n, k, :], AX.X, ALU.max), [padded])
            off = V("edge_off", lambda e, k=k, n=n: e.tensor_scalar(
                off_f[0:n, k, :], dst_i[0:n, k, :], ext[0:n, k, 0:1], None, ALU.subtract), [lo])
        turned_bank = {}
        copied = None
        for f, (name, o, s) in enumerate((("idx", idxT, idx_f), ("dst", dstT, dst_f), ("off", offT, off_f), ("nrm", nrmT, nrm_f))):
            for k, n in enumerate(BLOCK):
                b = 3 + (2 * f + k) % 2
                def make(e, s=s, k=k, n=n, b=b):
                    for j in range(CHUNKS):
                        m = e.transpose(bank[b][:, j * P:j * P + n], s[0:n, k, j * P:(j + 1) * P], ident[0:n, 0:n])
                    return m
                m = T("turn_edges", make, [off, consts] + ([turned_bank[b]] if b in turned_bank else []))
                turned_bank[b] = copied = V("edge_copy", lambda e, o=o, k=k, n=n, b=b: e.tensor_copy(
                    o[:, :, FIRST[k]:FIRST[k] + n],
                    bank[b][:, :].rearrange("p (j b) -> p j b", j=CHUNKS)[:, :, 0:n]), [m])
        def ext_rows(e):
            for i in range(2):
                for k, n in enumerate(BLOCK):
                    m = e.matmul(bank[3][0:1, i * 256 + FIRST[k]:i * 256 + FIRST[k] + n], ext[0:n, k, i:i + 1],
                                 ident[0:n, 0:n], start=True, stop=True)
            return m
        m = T("ext_rows", ext_rows, [copied])
        r = V("ext_copy", lambda e: e.tensor_copy(rows[0:1, 0:2, :], bank[3][0:1, :].rearrange(
            "p (i b) -> p i b", i=2)[:, :, 0:BATCHES]), [m])
        r0 = V("ext_copy", lambda e: e.tensor_copy(basei[:, :], bank[3][0:1, 0:BATCHES]), [m])

        def turn_wq(e):
            for j in range(PAIRS):
                for h in range(KH):
                    m = e.transpose(bank[1 + j // 2][:, (j % 2) * D + h * P:(j % 2) * D + (h + 1) * P],
                                    wq_s[:, h, j * P:(j + 1) * P], ident[:, :])
            return m
        m = T("turn_wq", turn_wq, [wq_in])
        for b in range(2):
            edge_lists_done = wqT_made = V("wqT", lambda e, b=b: e.tensor_copy(
                wqT[:, 2 * b:2 * b + 2, :], bank[1 + b][:, :].rearrange("p (j o) -> p j o", j=2)), [m])
        evacuated_start = wqT_made

        order, closed, emitted = [], [0] * BATCHES, 0

        def batches_to(n, groups):
            nonlocal emitted
            while emitted < min(n, BATCHES):
                closed[emitted] = groups * GROUP * P
                order.append(("batch", emitted))
                emitted += 1

        def enough(g):
            return BATCHES if (g + 1) * GROUP * P >= N else -(-(g + 1) * GROUP * P * E // N // BATCH) + LAG

        batches_to(enough(0), 0)
        order += [("open", 0), ("norm", 0), ("route", 0), ("choose", 0), ("up", 0, 0)]
        for g in range(GROUPS):
            for x_ in range(X):
                if g + 1 < GROUPS:
                    if x_ == X - 4:
                        batches_to(enough(g + 1), g + 1)
                        order.append(("open", g + 1))
                    if x_ == X - 3:
                        order.append(("norm", g + 1))
                    if x_ == X - 2:
                        order.append(("route", g + 1))
                    if x_ == X - 1:
                        order.append(("choose", g + 1))
                nxt = (g, x_ + 1) if x_ + 1 < X else (g + 1, 0)
                started = g + 1 + (x_ >= X - 4 and g + 1 < GROUPS)
                if nxt[0] < GROUPS:
                    order.append(("up", *nxt))
                batches_to(emitted + 1, started)
                order.append(("down", g, x_))
                batches_to(emitted + 1, started)
            order.append(("close", g))
        assert emitted == BATCHES

        b = 0
        while b < BATCHES:
            n = b
            while n < BATCHES and closed[n] == closed[b]:
                n += 1
            r1 = V("bounds", lambda e, b=b, n=n: e.memset(rows[0:1, 2, b:n], float(closed[b])))
            b = n
        q = V("even", lambda e: e.tensor_tensor(rows[0:1, 3, :], rows[0:1, 0, :], rows[0:1, 2, :], ALU.is_ge), [r, r1])
        q1 = V("even", lambda e: e.tensor_tensor(rows[0:1, 4, :], rows[0:1, 1, :], rows[0:1, 0, :], ALU.subtract), [r])
        q1 = V("even", lambda e: e.tensor_scalar(rows[0:1, 4, :], rows[0:1, 4, :], float(WINDOW), None, ALU.is_lt), [q1])
        q = V("even", lambda e: e.tensor_tensor(rows[0:1, 5, :], rows[0:1, 3, :], rows[0:1, 4, :], ALU.mult), [q1])
        q = V("even", lambda e: e.tensor_reduce(flag[:, 0:1], rows[0:1, 5, :], AX.X, ALU.min), [q])
        q = V("even", lambda e: e.tensor_scalar(flag[:, 1:2], flag[:, 0:1], -1.0, 1.0, ALU.mult, ALU.add), [q])
        slow_known = V("even", lambda e: e.tensor_copy(slowi[:, :], flag[:, 1:2]), [q])
        m = T("slow_all", lambda e: e.matmul(bank[4][:, 0:1], ones1[:, :], flag[:, 1:2], start=True, stop=True), [slow_known])
        q = V("mask", lambda e: e.tensor_scalar(slow_all[:, :], bank[4][:, 0:1], -float(2 * AGG), None, ALU.mult), [m])
        offsets = V("mask", lambda e: e.tensor_scalar(offT[:, :, :], offT[:, :, :], slow_all[:, 0:1], None, ALU.add), [q])

        kv_read[-1] = [offsets]
        for t in range(TILES):
            if t + 3 < TILES:
                load_x(t + 3)
            if t == 0:
                S.put("tensor", "pe_setup", lambda e: e.transpose(bank[5][:, 0:P], ident[:, :], ident[:, :]),
                      [offsets, evacuated_start])
            keys_values(t)
            head_squares(t)
            if t + 2 < TILES:
                ln_stats(t + 2)
                ln_sqrt(t + 2)
            head_vars(t)
            if t + 1 < TILES:
                turn(t + 1)
            messages(t, 0)
            evacuate(t, 0)
            messages(t, 1)
            evacuate(t, 1)
            if t + 1 < TILES:
                copy_turned(t + 1)
            head_scale(t)
            for n in range(2, 5):
                messages(t, n)
                evacuate(t, n)
            if t + 1 < TILES:
                gates(t + 1)
            if t + 2 < TILES:
                normalize(t + 2)
            for n in range(5, NB):
                messages(t, n)
                evacuate(t, n)
            if t + 1 < TILES:
                sigmoid(t + 1)
            dots(t)
            store(t)

        z = V("fold_zero", lambda e: e.memset(bd, 0.0), [stored[TILES - 1], stored[TILES - 2]])
        for q in range(2):
            half = slice(q * HEAD, (q + 1) * HEAD)
            s = V("fold_dots", lambda e, half=half: e.tensor_scalar(
                bd[half, :, half], bank[5][half, :].rearrange("p (j d) -> p j d", j=PAIRS)[:, :, half],
                1.0 / N, None, ALU.mult), [z, dots_done[TILES - 1]])

        def fold_out(e):
            for j in range(PAIRS):
                m = e.matmul(bank[3 + j // 2][:, (j % 2) * D:(j % 2 + 1) * D], bd[:, j, :], wout_s[:, j, :],
                             start=True, stop=True)
            return m
        m = T("fold_out", fold_out, [s, wout_in] + kv_read[TILES - 1])
        for b in range(2):
            s = V("fold_copy", lambda e, b=b: e.tensor_copy(
                fold[:, 2 * b:2 * b + 2, :], bank[3 + b][:, :].rearrange("p (j o) -> p j o", j=2)), [m])

        def fold_in(e):
            for h in range(KH):
                for j in range(PAIRS):
                    m = e.matmul(bank[0][:, h * D:(h + 1) * D], wqT[:, j, h * P:(h + 1) * P], fold[:, j, :],
                                 start=j == 0, stop=j == PAIRS - 1)
            return m
        m = T("fold_in", fold_in, [s] + evacuated[-3:])
        mix_made = V("mix", lambda e: e.tensor_copy(mix[:, :, :], bank[0][:, :].rearrange("p (h o) -> p h o", h=KH)), [m])
        agg_zero.append(V("lent_zero", lambda e: e.memset(agg[:, KH - 1, AGG - LENT:AGG], 0.0), [m]))
        agg_zero = [agg_zero[-2], agg_zero[-1]]
        table_in = [stored[TILES - 1], stored[TILES - 2]]
        phase_a = table_in + [mix_made]

        table_rows = table.rearrange("n (r o) -> (n r) o", r=R)
        g_free, g_idx, g_msg, g_oh, g_ps, g_add = (S.sem(f"general_{n}") for n in ("free", "idx", "msg", "onehot", "psum", "add"))
        from_pe, from_dve = bank[0], bank[0]

        def general_pool(e):
            slow = e.value_load(slowi[0:1, 0:1], min_val=0, max_val=1)
            with e.If(slow):
                with e.Fori(0, BATCHES) as b:
                    e.wait_ge(g_free, b + 1)
                    e.tensor_copy(idxG[:, :], idxT[:, :, bass.ds(b, 1)].rearrange("p j o -> p (j o)")).then_inc(g_idx, 1)
                    e.wait_ge(g_idx, b + 1)
                    e.tensor_tensor(carrier[:, :], carrier[:, :], carrier[:, :], ALU.add)
                    for j in range(CHUNKS):
                        e.indirect_dma_start(msg[:, 0, j, :], None, table_rows,
                                             bass.IndirectOffsetOnAxis(idxG[:, j:j + 1], 0)).then_inc(g_msg, 16)
                    e.wait_ge(g_msg, b * 16 * CHUNKS + 16 * CHUNKS)
                e.wait_ge(g_free, BATCHES + 1)

        def general_vector(e):
            slow = e.value_load(slowi[0:1, 0:1], min_val=0, max_val=1)
            with e.If(slow):
                e.sem_inc(g_free, 1)
                with e.Fori(0, BATCHES) as b:
                    e.tensor_copy(dstG.unsqueeze(2), dstT[:, :, bass.ds(b, 1)])
                    e.tensor_copy(nrmG.unsqueeze(2), nrmT[:, :, bass.ds(b, 1)]).then_inc(g_add, 1)
                    with e.Fori(0, TILES) as w:
                        e.wait_ge(g_add, b * (2 * TILES + 1) + 1)
                        for j in range(CHUNKS):
                            o = e.tensor_scalar(onehot[:, 0, j, :], iota[:, :], dstG[:, j:j + 1], nrmG[:, j:j + 1],
                                                ALU.is_equal, ALU.mult)
                        o.then_inc(g_oh, 1)
                        e.tensor_scalar(dstG, dstG, float(P), None, ALU.subtract).then_inc(g_add, 1)
                        e.wait_ge(g_add, b * (2 * TILES + 1) + w * 2 + 2)
                        e.wait_ge(g_ps, b * TILES + w + 1)
                        cols = agg[:, :, bass.ds(w * P, P)]
                        e.tensor_tensor(cols, cols, from_pe[:, 0:D].rearrange("p (h n) -> p h n", h=KH),
                                        ALU.add).then_inc(g_add, 1)
                        e.wait_ge(g_add, b * (2 * TILES + 1) + w * 2 + 3)
                    e.sem_inc(g_free, 1)

        def general_tensor(e):
            slow = e.value_load(slowi[0:1, 0:1], min_val=0, max_val=1)
            with e.If(slow):
                with e.Fori(0, BATCHES) as b:
                    with e.Fori(0, TILES) as w:
                        e.wait_ge(g_msg, b * 16 * CHUNKS + 16 * CHUNKS)
                        e.wait_ge(g_oh, b * TILES + w + 1)
                        for h in range(KH):
                            for j in range(CHUNKS):
                                m = e.matmul(from_dve[:, h * P:(h + 1) * P], msg[:, 0, j, h * P:(h + 1) * P],
                                             onehot[:, 0, j, :], start=j == 0, stop=j == CHUNKS - 1)
                        m.then_inc(g_ps, 1)

        S.put("gpsimd", None, general_pool, table_in + [slow_known, copied])
        S.put("vector", None, general_vector, phase_a + agg_zero + [slow_known])
        S.put("tensor", None, general_tensor, phase_a + [slow_known])

        gathered, hot, summed, added, base = {}, {}, {}, {}, {}

        def gather(b):
            after = ([summed[b - SLOTS]] if b >= SLOTS else table_in + [offsets])
            def make(e):
                for j in range(CHUNKS):
                    m = e.indirect_dma_start(msg[:, b % SLOTS, j, :], None, table_rows,
                                             bass.IndirectOffsetOnAxis(idxT[:, j, b:b + 1], 0))
                    if j < CHUNKS - 1:
                        m.then_inc(S.sem(f"gather{b % SLOTS}"), 16)
                return m
            S.put("gpsimd", f"gather{b % SLOTS}", make, after, by=16)
            S.value[f"gather{b % SLOTS}"] += 16 * (CHUNKS - 1)
            gathered[b] = (f"gather{b % SLOTS}", S.value[f"gather{b % SLOTS}"])

        def one_hot(b):
            def make(e):
                for j in range(CHUNKS):
                    m = e.tensor_scalar(onehot[:, b % 2, j, :], iota[:, :], offT[:, j, b:b + 1], nrmT[:, j, b:b + 1],
                                        ALU.is_equal, ALU.mult)
                return m
            hot[b] = V("onehot", make, ([summed[b - 2]] if b >= 2 else phase_a + [offsets]))

        def sum_batch(b):
            ps = bank[b % 2]
            def make(e):
                for h in range(KH):
                    for j in range(CHUNKS):
                        m = e.matmul(ps[:, h * P:(h + 1) * P], msg[:, b % SLOTS, j, h * P:(h + 1) * P],
                                     onehot[:, b % 2, j, :], start=j == 0, stop=j == CHUNKS - 1)
                return m
            summed[b] = T("sum_batch", make, [gathered[b], hot[b]] + ([added[b - 2]] if b >= 2 else phase_a))

        def add_batch(b):
            def make(e):
                if b % BASES == 0:
                    n = min(BASES, BATCHES - b)
                    _, values = nc.values_load_multi_w_load_instructions(
                        basei[0:1, b:b + n], engines=[e.engine], min_val=0, max_val=AGG - WINDOW,
                        skip_runtime_bounds_check_because="a destination is a node")
                    base.update({b + i: v for i, v in enumerate(values)})
                cols = agg[:, :, bass.ds(base[b], WINDOW)]
                return e.tensor_tensor(cols, cols, bank[b % 2][:, 0:D].rearrange("p (h n) -> p h n", h=KH), ALU.add)
            added[b] = V("add_batch", make, [summed[b], slow_known] + ([added[b - 1]] if b else []))

        def batch(b):
            if b == 0:
                for i in range(min(SLOTS, BATCHES)):
                    gather(i)
                one_hot(0)
            if b + 1 < BATCHES:
                one_hot(b + 1)
            sum_batch(b)
            if b + SLOTS < BATCHES:
                gather(b + SLOTS)
            add_batch(b)
            added_last[0] = added[b]

        added_last = [None]
        tiles_of = lambda g: min(GROUP, TILES - g * GROUP)
        group_in, xnT_in, x2_made, x2_read, acc_made = {}, {}, {}, {}, {}
        relu_read, x3_made, x3T_made, comb_made, store_out = {}, {}, {}, {}, {}
        opened, up_done, h_made, down_done, y_read, misc_read = {}, {}, {}, {}, [], []
        x3_turned, b2_read, up_last = {}, {}, {}

        def load_group(g):
            K = tiles_of(g)
            after = [opened[g - 2]] if g >= 2 else phase_a
            full = K if (g * GROUP + K) * P <= N else K - 1
            n0 = g * GROUP * P
            if full:
                group_in[g] = S.dma(f"group_x{g % 2}", x_g[:, g % 2, 0:full, :],
                                    x[n0:n0 + full * P, :].rearrange("(k p) o -> p k o", p=P), after)
            if full < K:
                group_in[g] = S.dma(f"group_x{g % 2}", x_g[0:LAST, g % 2, full, :], x[n0 + full * P:N, :], after)
            group_xnT = [xnT_stored[t] for t in range(g * GROUP, g * GROUP + K)]
            xnT_in[g] = S.dma(f"group_xnT{g % 2}", xnT_g[:, g % 2, :, 0:K * P], xnT_dram[g, :, :, 0:K * P], after + group_xnT)

        def open_group(g):
            s = g % 2
            for k in range(tiles_of(g)):
                t = g * GROUP + k
                for h in range(KH):
                    r = V("relu", lambda e, t=t, h=h: e.tensor_scalar(
                        relu[:, t % 2, h, :], agg[:, h, t * P:(t + 1) * P], 0.0, boutT[:, h:h + 1], ALU.max, ALU.add),
                        [added_last[0]] + ([relu_read[t - 2]] if t >= 2 else []))
                def make(e, t=t, k=k, s=s):
                    for h in range(KH):
                        e.matmul(bank[2][:, 0:D], xnT_g[:, s, h, k * P:(k + 1) * P], mix[:, h, :],
                                 start=h == 0, stop=False, skip_group_check=True)
                    for h in range(KH):
                        m = e.matmul(bank[2][:, h * P:(h + 1) * P], relu[:, t % 2, h, :], ident[:, :],
                                     start=False, stop=h == KH - 1, skip_group_check=True)
                    return m
                relu_read[t] = T("x2_sum", make, [r, xnT_in[g]] + ([x2_read[t - 1]] if t else []) + ([b2_read[g - 1]] if g else []))
                x2_read[t] = V("x2", lambda e, k=k, s=s: e.tensor_tensor(
                    acc[:, s, k, :], bank[2][:, 0:D], x_g[:, s, k, :], ALU.add),
                    [relu_read[t], group_in[g]] + ([store_out[g - 2]] if g >= 2 else []))
                q = V("x2_stats", lambda e, k=k, s=s: e.bn_stats(stB[:, k, 0:6], acc[:, s, k, :]), [x2_read[t]])
                q = V("x2_stats", lambda e, k=k: e.bn_aggr(mvB[:, k, :], stB[:, k, 0:6]), [q])
            opened[g] = x2_read[t]
            if g + 2 < GROUPS:
                load_group(g + 2)
            x2_made[g] = V("x2_stats", lambda e: e.tensor_scalar(
                sdB[:, 0, 0:tiles_of(g)].unsqueeze(2), mvB[:, 0:tiles_of(g), 1:2], EPS, None, ALU.add), [q])

        def norm_group(g):
            s, K = g % 2, tiles_of(g)
            q = A("x2_sqrt", lambda e: e.activation(sdB[:, 1, 0:K], sdB[:, 0, 0:K], ACT.Sqrt), [x2_made[g]])
            q = V("x2_rstd", lambda e: e.reciprocal(sdB[:, 2, 0:K], sdB[:, 1, 0:K]), [q])
            for k in range(K):
                x3_made[g, k] = V("x3", lambda e, k=k: e.tensor_scalar(
                    x3[:, k, :], acc[:, s, k, :], mvB[:, k, 0:1], sdB[:, 2, k:k + 1], ALU.subtract, ALU.mult),
                    [q] + ([x3_turned[g - 1]] if g else []))
            acc_made[g] = V("acc", lambda e: e.tensor_tensor(acc[:, s, 0:K, :], acc[:, s, 0:K, :], x3[:, 0:K, :], ALU.add),
                            [x3_made[g, K - 1]])
            for k in range(K):
                def make(e, k=k):
                    for h in range(KH):
                        m = e.transpose(bank[3][:, h * P:(h + 1) * P], x3[:, k, h * P:(h + 1) * P], ident[:, :])
                    return m
                x3_turned[g] = T("turn_x3", make, [x3_made[g, k]] + misc_read[-1:])
                x3T_made[g] = A("x3T", lambda e, k=k: e.copy(
                    x3T[:, s, :, k * P:(k + 1) * P], bank[3][:, 0:D].rearrange("p (h n) -> p h n", h=KH)),
                    [x3_turned[g]] + ([up_last[g - 2]] if g >= 2 else []))
                misc_read.append(x3T_made[g])

        def route_group(g):
            s, K = g % 2, tiles_of(g)
            def make(e):
                for k in range(K):
                    for h in range(KH):
                        m = e.matmul(bank[3][:, k * X:(k + 1) * X], x3T[:, s, h, k * P:(k + 1) * P],
                                     routerT[:, h * X:(h + 1) * X], start=h == 0, stop=h == KH - 1)
                return m
            m = T("logits", make, [x3T_made[g]])
            lg = bank[3][:, 0:K * X].rearrange("p (k x) -> p k x", x=X)
            wide = lambda v: v.unsqueeze(2).to_broadcast([P, K, X])
            q = V("softmax", lambda e: e.tensor_reduce(smB[:, 0, 0:K], lg, AX.X, ALU.max), [m])
            q = V("softmax", lambda e: e.tensor_tensor(lgB[:, 0, 0:K, :], lg, wide(smB[:, 0, 0:K]), ALU.subtract), [q])
            misc_read.append(q)
            q = A("exp", lambda e: e.activation(lgB[:, 1, 0:K, :], lgB[:, 0, 0:K, :], ACT.Exp), [q])
            q = V("softmax", lambda e: e.tensor_reduce(smB[:, 1, 0:K], lgB[:, 1, 0:K, :], AX.X, ALU.add), [q])
            q = V("softmax", lambda e: e.reciprocal(smB[:, 2, 0:K], smB[:, 1, 0:K]), [q])
            comb_made[g] = V("softmax", lambda e: e.tensor_tensor(
                lgB[:, 2, 0:K, :], lgB[:, 1, 0:K, :], wide(smB[:, 2, 0:K]), ALU.mult), [q])

        def choose_group(g):
            s, K = g % 2, tiles_of(g)
            q = comb_made[g]
            for k in range(K):
                q1 = V("top2", lambda e, k=k: e.max(topB[:, k, :], lgB[:, 2, k, :]), [q])
            for k in range(K):
                q2 = V("top2", lambda e, k=k: e.max_index(topi[:, k, :], topB[:, k, :], lgB[:, 2, k, :]), [q1])
            q = V("top2", lambda e: e.tensor_tensor(smB[:, 3, 0:K].unsqueeze(2), topB[:, 0:K, 0:1], topB[:, 0:K, 1:2], ALU.add), [q1])
            q = V("top2", lambda e: e.tensor_scalar(smB[:, 4, 0:K], smB[:, 3, 0:K], 1e-12, None, ALU.max), [q])
            q = V("top2", lambda e: e.reciprocal(smB[:, 5, 0:K], smB[:, 4, 0:K]), [q])
            V("top2", lambda e: e.tensor_copy(wB[:, 1, 0:K, :], topi[:, 0:K, 0:2]), [q2])
            q = V("top2", lambda e: e.tensor_tensor(wB[:, 0, 0:K, :], topB[:, 0:K, 0:2],
                                                    smB[:, 5, 0:K].unsqueeze(2).to_broadcast([P, K, 2]), ALU.mult), [q])
            for k in range(K):
                for i, o in ((0, combB[:, s, k, :]), (1, c2B[:, 0, k, :])):
                    q1 = V("top2", lambda e, k=k, i=i, o=o: e.tensor_scalar(
                        o, iota[:, 0:X], wB[:, 1, k, i:i + 1], wB[:, 0, k, i:i + 1], ALU.is_equal, ALU.mult),
                        [q] + ([down_done[g - 2, X - 1]] if g >= 2 else []))
            comb_made[g] = V("top2", lambda e: e.tensor_tensor(combB[:, s, 0:K, :], combB[:, s, 0:K, :], c2B[:, 0, 0:K, :], ALU.add), [q1])
            def make(e):
                for k in range(K):
                    m = e.matmul(bank[2][0:X, k * P:(k + 1) * P], combB[:, s, k, :], ident[:, :], start=True, stop=True)
                return m
            m = T("turn_comb", make, [comb_made[g], opened[g]])
            q = A("combT", lambda e: e.copy(combT[0:X, 0:K * P], bank[2][0:X, 0:K * P]), [m] + ([b2_read[g - 1]] if g else []))
            for k in range(K):
                m = T("b2_sum", lambda e, k=k: e.matmul(bank[2][:, 0:D], combT[0:X, k * P:(k + 1) * P], b2_s[:, :],
                                                        start=True, stop=True), [q, experts_in] + ([b2r] if k else []))
                b2r = V("b2_add", lambda e, k=k: e.tensor_tensor(acc[:, s, k, :], bank[2][:, 0:D], acc[:, s, k, :], ALU.add),
                        [m, acc_made[g]])
            b2_read[g] = acc_made[g] = b2r

        ups = [0]

        def up(g, x_):
            s, n = g % 2, tiles_of(g) * P
            for f in range(KH):
                i = ups[0]
                ups[0] += 1
                def make(e, f=f, i=i):
                    for h in range(KH):
                        m = e.matmul(bank[4 + i % 2][:, 0:n], w1_s[:, h, x_, f * P:(f + 1) * P], x3T[:, s, h, 0:n],
                                     start=h == 0, stop=h == KH - 1)
                    return m
                m = T("up", make, [x3T_made[g], experts_in] + ([h_made[i - 2]] if i >= 2 else []))
                up_last[g] = m
                after = [m] + ([down_order[-1]] if down_order else [])
                h_made[i] = A("h", lambda e, f=f, i=i: e.activation(
                    h_s[:, (i // 2) % 2, f, 0:n], bank[4 + i % 2][:, 0:n], ACT.Gelu,
                    bias=b1T[:, x_ * KH + f:x_ * KH + f + 1]), after)
            h_of[g, x_] = (h_made[i], (i // 2) % 2)

        h_of, down_order = {}, []

        def down(g, x_):
            s = g % 2
            made, hslot = h_of[g, x_]
            for k in range(tiles_of(g)):
                i = len(y_read)
                def make(e, k=k, i=i):
                    for f in range(KH):
                        m = e.matmul(bank[6 + i % 2][:, 0:D], h_s[:, hslot, f, k * P:(k + 1) * P], w2_s[:, f, x_, :],
                                     start=f == 0, stop=f == KH - 1)
                    return m
                m = T("down", make, [made] + ([y_read[i - 2]] if i >= 2 else []))
                y_read.append(V("y_add", lambda e, k=k, i=i: e.scalar_tensor_tensor(
                    acc[:, s, k, :], bank[6 + i % 2][:, 0:D], combB[:, s, k, x_:x_ + 1], acc[:, s, k, :], ALU.mult, ALU.add),
                    [m, comb_made[g], y_read[-tiles_of(g)] if x_ else acc_made[g]]))
            down_order.append(m)
            down_done[g, x_] = y_read[-1]

        def close_group(g):
            s, K = g % 2, tiles_of(g)
            full = K if (g * GROUP + K) * P <= N else K - 1
            n0 = g * GROUP * P
            if full:
                store_out[g] = S.dma(f"out_store{s}", out[n0:n0 + full * P, :].rearrange("(k p) o -> p k o", p=P),
                                     acc[:, s, 0:full, :], [y_read[-1]])
            if full < K:
                store_out[g] = S.dma(f"out_store{s}", out[n0 + full * P:N, :], acc[0:LAST, s, full, :], [y_read[-1]])

        load_group(0)
        load_group(1)
        steps = {"batch": batch, "open": open_group, "norm": norm_group, "route": route_group,
                 "choose": choose_group, "up": up, "down": down, "close": close_group}
        for name, *args in order:
            steps[name](*args)
        finals = {s: v for s, v in S.value.items() if s.startswith(("out_store", "table_store", "xnT_store"))}

        block = ctx.enter_context(nc.Block())

        @block.sync
        def _(eng):
            for emit in S.queue["sync"]:
                emit(eng)
            for name, value in finals.items():
                eng.wait_ge(S.sem(name), value)

        @block.scalar
        def _(eng):
            for emit in S.queue["scalar"]:
                emit(eng)

        @block.vector
        def _(eng):
            for emit in S.queue["vector"]:
                emit(eng)

        @block.gpsimd
        def _(eng):
            for emit in S.queue["gpsimd"]:
                emit(eng)

        @block.tensor
        def _(eng):
            for emit in S.queue["tensor"]:
                emit(eng)


_INS = ["x", "src", "dst", "edge_type_16", "edge_weight1", "L0_gnn_weight", "L0_gnn_gate_weight", "L0_mix_w_qkv",
        "L0_mix_w_out", "L0_mix_b_out", "L0_ffn_router_w", "L0_ffn_w1", "L0_ffn_b1", "L0_ffn_w2", "L0_ffn_b2"]


def kernel(**inputs):
    import numpy as np
    import concourse.bacc as bacc
    from concourse.bass_utils import run_bass_kernel_spmd as run

    nc = bacc.Bacc("TRN2", target_bir_lowering=False, num_devices=1)
    arrays, args = {}, []
    for name in _INS:
        a = np.ascontiguousarray(inputs[name])
        arrays[f"in_{name}"] = a
        args.append(nc.dram_tensor(f"in_{name}", a.shape, mybir.dt.from_np(a.dtype), kind="ExternalInput").ap())
    shape = arrays["in_x"].shape
    args.append(nc.dram_tensor("out_dram", shape, F32, kind="ExternalOutput").ap())
    gps_layer(nc, *args)
    r = run(nc, [arrays], core_ids=[0])
    return r.results[0]["out_dram"]
```

```python
from contextlib import ExitStack

import concourse.bass as bass
from concourse import mybir

F32 = mybir.dt.float32
F32R = mybir.dt.float32r
I32 = mybir.dt.int32
U32 = mybir.dt.uint32
ALU = mybir.AluOpType
ACT = mybir.ActivationFunctionType
AX = mybir.AxisListType

P = 128
EPS = 1e-5
BANK = 512
CHUNKS = 4
BATCH = CHUNKS * P
WINDOW = P
GROUP = 4
AHEAD = 7
FIRST_PIECE = 9
LAG = 3
BASES = 8


class Streams:

    def __init__(self, nc, ctx):
        self.nc, self.ctx = nc, ctx
        self.queue = {e: [] for e in ("sync", "scalar", "vector", "gpsimd", "tensor")}
        self.sems, self.value, self.seen = {}, {}, {}

    def sem(self, name):
        if name not in self.sems:
            self.sems[name] = self.ctx.enter_context(self.nc.semaphore("s_" + name))
            self.value[name] = 0
        return self.sems[name]

    def put(self, engine, step, make, after=(), by=1):
        waits = []
        for name, value in after:
            if self.seen.get((engine, name), 0) < value:
                self.seen[engine, name] = value
                waits.append((self.sem(name), value))
        sem = self.sem(step) if step else None

        def emit(eng):
            for s, value in waits:
                eng.wait_ge(s, value)
            made = make(eng)
            if sem is not None:
                made.then_inc(sem, by)

        self.queue[engine].append(emit)
        if not step:
            return None
        self.value[step] += by
        return step, self.value[step]

    def dma(self, step, out, in_, after=(), engine="sync"):
        return self.put(engine, step, lambda e: e.dma_start(out, in_), after, by=16)


def gps_layer(nc, x, src, dst, rel, norm, w_rel, w_gate, w_qkv, w_out, b_out, w_router, w1, b1, w2, b2, out):
    N, D = x.shape
    E = src.shape[0]
    R = w_rel.shape[0]
    X = w1.shape[0]
    INNER = w_out.shape[0]
    HEAD = 64
    KH = D // P
    PAIRS = INNER // P
    VK = 2 * INNER
    TILES = -(-N // P)
    LAST = N - (TILES - 1) * P
    GROUPS = -(-TILES // GROUP)
    SIZE = [GROUP] * GROUPS
    for g in range(GROUPS * GROUP - TILES):
        SIZE[GROUPS - 1 - g] -= 1
    START = [sum(SIZE[:g]) for g in range(GROUPS + 1)]
    PLACE = [(g, k) for g in range(GROUPS) for k in range(SIZE[g])]
    BATCHES = -(-E // BATCH)
    TAIL = E - (BATCHES - 1) * BATCH
    BLOCK = (BATCHES - 97, 97)
    FIRST = (0, BLOCK[0])
    assert D == 2 * P and D % P == 0 and BLOCK[0] <= P and E % BATCH and R * D % BANK == 0
    NB = R * D // BANK
    PER = BANK // D
    AGG = TILES * P + WINDOW

    ctx = ExitStack()
    with ctx:
        S = Streams(nc, ctx)

        def sb(name, shape, dt=F32):
            return ctx.enter_context(nc.sbuf_tensor(name, shape, dt))

        bank = [ctx.enter_context(nc.psum_tensor(f"bank{i}", [P, BANK], F32)) for i in range(8)]
        table = nc.dram_tensor("messages", [N, R * D], F32, kind="Internal").ap()
        xnT_dram = nc.dram_tensor("xnT_scratch", [GROUPS, P, 2, KH, GROUP * P], F32, kind="Internal").ap()

        ident = sb("ident", [P, P])
        iota = sb("iota", [P, P])
        small = sb("small", [P, 96])
        gateT, routerT = small[:, 0:2 * R], small[:, 2 * R:2 * R + 2 * X]
        boutT = small[:, 2 * R + 2 * X:2 * R + 2 * X + KH]
        b1T = small[:, 64:64 + KH * X]
        idxT = sb("idxT", [P, CHUNKS, BATCHES], I32)
        offT = sb("offT", [P, CHUNKS, BATCHES])
        nrmT = sb("nrmT", [P, CHUNKS, BATCHES])
        basei = sb("basei", [1, BATCHES], I32)
        carrier = sb("carrier", [P, 1], I32)
        slowi = sb("slowi", [1, 1], I32)
        flag = sb("flag", [1, 8])
        slow_all = sb("slow_all", [P, 1])
        ones1 = sb("ones1", [1, P])
        topi = sb("topi", [P, GROUP, 8], U32)
        general_lists = sb("general_lists", [P, 2, CHUNKS])
        dstG, nrmG = general_lists[:, 0, :], general_lists[:, 1, :]
        idxG = sb("idxG", [P, CHUNKS], I32)

        class Arena:

            def __init__(self, name, words, dt):
                self.whole, self.words, self.at = sb(name, [P, words], dt), words, 0

            def carve(self, *shape):
                n = 1
                for d in shape:
                    n *= d
                assert self.at + n <= self.words, (self.at, n)
                v = self.whole[:, self.at:self.at + n]
                self.at += n
                names = " ".join("abcd"[:len(shape)])
                if len(shape) > 1:
                    v = v.rearrange(f"p ({names}) -> p {names}", **dict(zip("abcd", shape)))
                return v

        parts = Arena("parts", 28848, F32R)
        w_p = parts.carve(2, KH, R * D)
        wkv_p = parts.carve(2, KH, VK)
        xnT_p = parts.carve(3, 2, KH, P)
        parts.at = wkv_at = 2 * KH * R * D + 2 * KH * VK
        xnT_kv = parts.carve(2, 2, KH, GROUP * P)
        mix_p = parts.carve(2, KH, D)
        piece_at = parts.at
        xnT_g = parts.carve(2, KH, GROUP * P)
        combT = parts.carve(GROUP * P)
        b2_p = parts.carve(2, D)
        pick = parts.carve(X)
        comb_p = parts.carve(GROUP, 2, X)
        gate_p = parts.carve(KH, 2, R)
        route_p = parts.carve(KH, 2, X)
        parts.at = piece_at
        piece_p = parts.carve(2, 2, BANK)
        parts.at = 0
        w1_p = parts.carve(2, KH, X, D)
        w2_p = parts.carve(2, KH, X, D)
        x3T = parts.carve(2, 2, KH, GROUP * P)
        h_p = parts.carve(2, 2, KH, GROUP * P)
        raw = lambda v: v.bitcast(F32)

        plain = Arena("plain", 23000, F32)
        stage = plain.carve(2, R, D)
        plain.at = 0
        w_raw = plain.carve(KH, R * D)
        lists_f = [plain.carve(2, BATCH) for _ in range(4)]
        idx_f, dst_f, off_f, nrm_f = lists_f
        lists_i = [plain.carve(2, BATCH).bitcast(I32) for _ in range(3)]
        src_i, dst_i, rel_i = lists_i
        dstT = plain.carve(CHUNKS, BATCHES)
        wkv_raw = plain.carve(KH, VK)
        ext = plain.carve(2, 2)
        wmean = plain.carve(KH * VK // HEAD)
        rows = plain.carve(6, BATCHES)
        x_ring = plain.carve(4, D)
        xn_ring = plain.carve(2, D)
        gate_ring = plain.carve(2, R)
        stA = plain.carve(2, 8)
        mvA = plain.carve(2, 4)
        wq_s = lists_f[0]
        piece_raw = lists_f[1]
        assert wq_s.shape[1] * wq_s.shape[2] == KH * INNER
        wqT_a = lists_f[2].rearrange("p a b -> p (a b)").rearrange("p (j o) -> p j o", j=PAIRS)
        iota_i = plain.carve(P).bitcast(I32)
        small_rows = plain.carve(2, BANK)
        SLOTS, HOTS = 4, 3
        plain.at = 0
        agg = plain.carve(KH, AGG)
        msg = plain.carve(SLOTS, CHUNKS, D)
        onehot = plain.carve(HOTS, CHUNKS, WINDOW)
        rest_at = plain.at
        sq = plain.carve(VK)
        v_s = plain.carve(2, INNER)
        k_s = plain.carve(2, INNER)
        wout_s = plain.carve(PAIRS, D)
        plain.at = rest_at
        wqT = plain.carve(PAIRS, D)
        bd = plain.carve(PAIRS, P)
        fold = plain.carve(PAIRS, D)
        dstL = msg[:, SLOTS - 1, :, :].rearrange("p j o -> p (j o)")[:, 0:CHUNKS * BATCHES].rearrange(
            "p (j b) -> p j b", j=CHUNKS)
        plain.at = rest_at
        acc = plain.carve(2, GROUP, D)
        x3 = plain.carve(2, D)
        g_s = plain.carve(KH, GROUP * P)
        xT = plain.carve(GROUP * P)
        hs = plain.carve(6, 2 * INNER // HEAD)
        stB = plain.carve(GROUP, 8)
        mvB = plain.carve(GROUP, 2)
        sdB = plain.carve(4, GROUP)
        lgB = plain.carve(3, GROUP, X)
        topB = plain.carve(GROUP, 8)
        smB = plain.carve(8, GROUP)
        wB = plain.carve(2, GROUP, 2)
        combB = plain.carve(2, GROUP, X)

        dst_dram = nc.dram_tensor("dst_scratch", [P, CHUNKS, BATCHES], F32, kind="Internal").ap()
        wqT_dram = nc.dram_tensor("wqT_scratch", [P, PAIRS, D], F32, kind="Internal").ap()
        w1_dram, w2_dram = (nc.dram_tensor(f"{n}_parts", [P, 2, KH, X * D], F32, kind="Internal").ap()
                            for n in ("w1", "w2"))

        V = lambda step, make, after=(): S.put("vector", step, make, after)
        A = lambda step, make, after=(): S.put("scalar", step, make, after)
        T = lambda step, make, after=(): S.put("tensor", step, make, after)
        G = lambda step, make, after=(): S.put("gpsimd", step, make, after)

        gate_rows, router_rows = small_rows[0:R, 0, 0:D], small_rows[0:X, 0, D:2 * D]
        bout_rows, b1_rows = small_rows[0:KH, 1, 0:P], small_rows[0:KH * X, 1, P:2 * P]
        b2_rows = small_rows[0:2 * X, 1, D:2 * D]

        def three(e, out, left, right, start, stop, **kw):
            e.matmul(out, left(0), right(0), start=start, stop=False, **kw)
            e.matmul(out, left(0), right(1), start=False, stop=False, **kw)
            return e.matmul(out, left(1), right(0), start=False, stop=stop, **kw)

        def tile_rows(t):
            return P if t < TILES - 1 else LAST

        x_loaded = {}

        def load_x(t):
            after = [xn_made[t - 4]] if t >= 4 else []
            if tile_rows(t) < P:
                z = V("x_pad", lambda e: e.memset(x_ring[:, t % 4, :], 0.0), after)
                after = after + [z]
            n = tile_rows(t)
            x_loaded[t] = S.dma(f"x_load{t % 4}", x_ring[0:n, t % 4, :], x[t * P:t * P + n, :], after)

        xn_made = {}
        for t in range(3):
            load_x(t)
        z = G("pool_const", lambda e: e.memset(ident[:, :], 0.0))
        z = G("pool_const", lambda e: e.affine_select(
            out=ident[:, :], in_=ident[:, :], compare_op=ALU.not_equal, fill=1.0, base=0,
            pattern=[[-1, P]], channel_multiplier=1), [z])
        z = G("pool_const", lambda e: e.iota(iota_i, pattern=[[1, P]], base=0, channel_multiplier=0), [z])
        z = G("pool_const", lambda e: e.tensor_copy(iota[:, :], iota_i), [z])
        z = G("pool_const", lambda e: e.memset(carrier[:, :], 0), [z])
        consts = G("pool_const", lambda e: e.memset(ones1[:, :], 1.0), [z])
        for o, i in ((gate_rows, w_gate.rearrange("r f a -> r (f a)")), (router_rows, w_router),
                     (bout_rows, b_out.rearrange("(h p) -> h p", p=P)),
                     (b1_rows, b1.rearrange("x (h p) -> (x h) p", p=P)), (b2_rows[0:X], b2), (b2_rows[X:2 * X], b2)):
            rows_in = S.dma("rows_in", o, i, engine="gpsimd")
        w_in = {}
        for n in range(NB):
            for k in range(KH):
                w_in[n, k] = S.dma(f"w_in{n}", w_raw[:, k, n * BANK:(n + 1) * BANK].rearrange("p (r o) -> p r o", o=D),
                                   w_rel[n * PER:(n + 1) * PER, k * P:(k + 1) * P, :].rearrange("r p o -> p r o"))
        edges_in = []
        for a, t in zip((src, dst, rel, norm.rearrange("e a -> (e a)")), (src_i, dst_i, rel_i, nrm_f)):
            n0, n1 = BLOCK[0] * BATCH, (BATCHES - 1) * BATCH
            for o, i in ((t[0:BLOCK[0], 0, :], a[0:n0].rearrange("(b e) -> b e", e=BATCH)),
                         (t[0:BLOCK[1] - 1, 1, :], a[n0:n1].rearrange("(b e) -> b e", e=BATCH)),
                         (t[BLOCK[1] - 1:BLOCK[1], 1, 0:TAIL], a[n1:E].rearrange("(b e) -> b e", b=1))):
                edges_in.append(S.dma("edges_in", o, i, engine="gpsimd"))
        edges_in = edges_in[-1]
        wkv_in = S.dma("wkv_in", wkv_raw, w_qkv[:, INNER:].rearrange("(k p) c -> p k c", p=P))

        def split(step, out, of, after_high, after_low=(), engine="scalar"):
            high = A(step + "_high", lambda e: e.copy(out(0), of), after_high)
            return high, V(step + "_low", lambda e: e.tensor_tensor(out(1), of, raw(out(0)), ALU.subtract),
                           [high, *after_low])

        pick_made = V("pick", lambda e: e.tensor_tensor(pick[0:2 * X, :], ident[0:2 * X, 0:X],
                                                        ident[0:2 * X, X:2 * X], ALU.add), [consts])
        def turn_small(e):
            for h in range(KH):
                e.transpose(bank[7][:, h * R:(h + 1) * R], gate_rows[:, h * P:(h + 1) * P], ident[0:R, 0:R])
                e.transpose(bank[7][:, 2 * R + h * X:2 * R + (h + 1) * X], router_rows[:, h * P:(h + 1) * P],
                            ident[0:X, 0:X])
            e.transpose(bank[7][:, 2 * R + 2 * X:2 * R + 2 * X + KH], bout_rows[:, :], ident[0:KH, 0:KH])
            return e.transpose(bank[7][:, 64:64 + KH * X], b1_rows[:, :], ident[0:KH * X, 0:KH * X])

        w_split = {}

        def split_w(n):
            for k in range(KH):
                c = slice(n * BANK, (n + 1) * BANK)
                w_split[n] = split("w", lambda i, k=k, c=c: w_p[:, i, k, c], w_raw[:, k, c], [w_in[n, KH - 1]])

        def center_kv():
            heads = VK // HEAD
            wkv_h = wkv_raw.rearrange("p k (h d) -> p (k h) d", d=HEAD)
            c = V("center", lambda e: e.tensor_reduce(wmean, wkv_h, AX.X, ALU.add), [wkv_in])
            c = V("center", lambda e: e.tensor_scalar(wmean, wmean, 1.0 / HEAD, None, ALU.mult), [c])
            c = V("center", lambda e: e.tensor_tensor(
                wkv_h, wkv_h, wmean.unsqueeze(2).to_broadcast([P, KH * heads, HEAD]), ALU.subtract), [c])
            return split("wkv", lambda i: wkv_p[:, i, :, :], wkv_raw, [c])

        kv_in, kv_done = {}, {}

        def load_kv(g, after):
            n = SIZE[g] * P
            kv_in[g] = S.dma(f"kv_in{g % 2}", raw(xnT_kv[:, (g + 1) % 2, :, :, :])[:, :, :, 0:n],
                             xnT_dram[g, :, :, :, 0:n], after)

        slot = lambda t, n: t % n
        ln_var, ln_sd = {}, {}

        def ln_stats(t):
            i = slot(t, 2)
            s = V("ln_stats", lambda e: e.bn_stats(stA[:, i, 0:6], x_ring[:, t % 4, :]), [x_loaded[t]])
            s = V("ln_stats", lambda e: e.bn_aggr(mvA[:, i, 0:2], stA[:, i, 0:6]), [s])
            ln_var[t] = V("ln_stats", lambda e: e.tensor_scalar(mvA[:, i, 2:3], mvA[:, i, 1:2], EPS, None, ALU.add), [s])

        def ln_sqrt(t):
            i = slot(t, 2)
            ln_sd[t] = A("ln_sqrt", lambda e: e.activation(mvA[:, i, 3:4], mvA[:, i, 2:3], ACT.Sqrt), [ln_var[t]])

        turned, xnT_made, xnT_stored, gates_done, gate_made = {}, {}, {}, {}, {}
        table_read, kv_read, stored, evacuated = {}, {}, {}, []

        def normalize(t):
            i = slot(t, 2)
            r = V("ln_rstd", lambda e: e.reciprocal(mvA[:, i, 3:4], mvA[:, i, 3:4]), [ln_sd[t]])
            xn_made[t] = V("xn", lambda e: e.tensor_scalar(
                xn_ring[:, i, :], x_ring[:, t % 4, :], mvA[:, i, 0:1], mvA[:, i, 3:4], ALU.subtract, ALU.mult),
                [r] + ([turned[t - 2]] if t >= 2 else []))

        def turn(t):
            def make(e):
                for h in range(KH):
                    m = e.transpose(bank[6][:, h * P:(h + 1) * P], xn_ring[:, t % 2, h * P:(h + 1) * P], ident[:, :])
                return m
            turned[t] = T("turn_xn", make, [xn_made[t], consts] + ([xnT_made[t - 1]] if t else []))

        def copy_turned(t):
            after = [turned[t]] + ([table_read[t - 3], xnT_stored[t - 3]] if t >= 3 else [])
            xnT_high, xnT_made[t] = split("xnT", lambda i: xnT_p[:, t % 3, i, :, :],
                                          bank[6][:, 0:D].rearrange("p (h n) -> p h n", h=KH), after)
            g, k = PLACE[t]
            for i in range(2):
                xnT_stored[t] = S.dma(f"xnT_store{t % 3}", xnT_dram[g, :, i, :, k * P:(k + 1) * P],
                                      raw(xnT_p[:, t % 3, i, :, :]), [xnT_high, xnT_made[t]])

        def gates(t):
            def make(e):
                for h in range(KH):
                    for i in range(2):
                        m = e.matmul(bank[7][:, 0:2 * R], xnT_p[:, t % 3, i, h, :], gate_p[:, h, :, :].rearrange("p i r -> p (i r)"),
                                     start=h == i == 0, stop=h == KH - 1 and i == 1)
                return m
            m = T("gates", make, [xnT_made[t], gate_split, gate_made[t - 1]])
            q = V("gate_low", lambda e: e.tensor_copy(gate_ring[:, t % 2, :], bank[7][:, R:2 * R]),
                  [m] + (evacuated[(t - 1) * NB - 2:(t - 1) * NB] if t >= 2 else []))
            gates_done[t] = V("gate_sum", lambda e: e.tensor_tensor(
                gate_ring[:, t % 2, :], gate_ring[:, t % 2, :], bank[7][:, 0:R], ALU.add), [q])

        def sigmoid(t):
            gate_made[t] = A("gate", lambda e: e.activation(gate_ring[:, t % 2, :], gate_ring[:, t % 2, :], ACT.Sigmoid),
                             [gates_done[t]])

        table_bank = {}

        MB = 5

        def messages(t, n):
            i = t * NB + n
            def make(e):
                for h in range(KH):
                    m = three(e, bank[i % MB][:, :], lambda q: xnT_p[:, t % 3, q, h, :],
                              lambda q: w_p[:, q, h, n * BANK:(n + 1) * BANK], h == 0, h == KH - 1)
                return m
            table_bank[i] = T("messages", make, [xnT_made[t], w_split[n][1]] + (
                [evacuated[i - MB]] if i >= MB else []))
            table_read[t] = table_bank[i]

        def evacuate(t, n):
            i = t * NB + n
            after = [table_bank[i], gate_made[t]] + ([stored[t - 2]] if t >= 2 else [w_split[i][1] for i in range(NB)])
            for r in range(PER):
                o = stage[:, t % 2, n * PER + r, :]
                s = bank[i % MB][:, r * D:(r + 1) * D]
                g = gate_ring[:, t % 2, n * PER + r:n * PER + r + 1]
                if n % 2:
                    done = A("stage_act", lambda e, o=o, s=s, g=g: e.activation(o, s, ACT.Copy, scale=g), after)
                else:
                    done = V("stage_dve", lambda e, o=o, s=s, g=g: e.tensor_scalar(o, s, g, None, ALU.mult), after)
            evacuated.append(done)

        def store(t):
            n = tile_rows(t)
            stored[t] = S.dma(f"table_store{t % 2}", table[t * P:t * P + n, :],
                              stage[0:n, t % 2, :, :].rearrange("p r o -> p (r o)"), evacuated[-2:])

        for t in range(2):
            ln_stats(t)
            ln_sqrt(t)
            normalize(t)
        turn(0)
        copy_turned(0)
        for n in range(NB):
            split_w(n)

        for n in range(3):
            messages(0, n)
        t_small = T("turn_small", turn_small, [consts, rows_in])
        small_in = V("small_copy", lambda e: e.tensor_copy(small[:, 0:2 * R + 2 * X + KH],
                                                           bank[7][:, 0:2 * R + 2 * X + KH]), [t_small])
        small_in = V("small_copy", lambda e: e.tensor_copy(b1T, bank[7][:, 64:64 + KH * X]), [t_small])
        gate_made[-1] = small_in
        gate_split = split("gate_w", lambda i: gate_p[:, :, i, :], gateT.rearrange("p (h r) -> p h r", h=KH), [small_in])[1]
        route_split = split("route_w", lambda i: route_p[:, :, i, :], routerT.rearrange("p (h r) -> p h r", h=KH), [small_in])[1]
        b2_made = split("b2", lambda i: b2_p[0:2 * X, i, :], b2_rows, [rows_in])[1]
        gates(0)
        sigmoid(0)

        last = BLOCK[1] - 1
        edge = {"read": []}

        def edge_rows(k):
            n = BLOCK[k]
            if k == 0:
                for t in (src_i, dst_i, rel_i):
                    V("edge_pad", lambda e, t=t: e.tensor_copy(
                        t[last:last + 1, 1, TAIL:BATCH], t[last:last + 1, 1, TAIL - 1:TAIL].to_broadcast([1, BATCH - TAIL])), [edges_in])
                edge["pad"] = V("edge_pad", lambda e: e.memset(nrm_f[last:last + 1, 1, TAIL:BATCH], 0.0), [edges_in])
            V("edge_idx", lambda e: e.scalar_tensor_tensor(
                idx_f[0:n, k, :], src_i[0:n, k, :], float(R), rel_i[0:n, k, :], ALU.mult, ALU.add), [edge["pad"]])
            V("edge_dst", lambda e: e.tensor_copy(dst_f[0:n, k, :], dst_i[0:n, k, :]), [edge["pad"]])
            lo = V("edge_ext", lambda e: e.tensor_reduce(ext[0:n, k, 0:1], dst_i[0:n, k, :], AX.X, ALU.min), [edge["pad"]])
            V("edge_ext", lambda e: e.tensor_reduce(ext[0:n, k, 1:2], dst_i[0:n, k, :], AX.X, ALU.max), [edge["pad"]])
            edge["off"] = V("edge_off", lambda e: e.tensor_scalar(
                off_f[0:n, k, :], dst_i[0:n, k, :], ext[0:n, k, 0:1], None, ALU.subtract), [lo])

        def edge_turn(o, s, k):
            n = BLOCK[k]
            def make(e):
                for j in range(CHUNKS):
                    m = e.transpose(bank[5][:, j * P:j * P + n], s[0:n, k, j * P:(j + 1) * P], ident[0:n, 0:n])
                return m
            m = T("turn_edges", make, [edge["off"], consts] + edge["read"])
            edge["read"] = [V("edge_copy", lambda e: e.tensor_copy(
                o[:, :, FIRST[k]:FIRST[k] + n],
                bank[5][:, :].rearrange("p (j b) -> p j b", j=CHUNKS)[:, :, 0:n]), [m])]
            edge["copied"] = edge["read"][0]

        def edge_ext():
            def make(e):
                for i in range(2):
                    for k, n in enumerate(BLOCK):
                        m = e.matmul(bank[5][0:1, i * 256 + FIRST[k]:i * 256 + FIRST[k] + n], ext[0:n, k, i:i + 1],
                                     ident[0:n, 0:n], start=True, stop=True)
                return m
            m = T("ext_rows", make, edge["read"])
            edge["ext"] = V("ext_copy", lambda e: e.tensor_copy(rows[0:1, 0:2, :], bank[5][0:1, :].rearrange(
                "p (i b) -> p i b", i=2)[:, :, 0:BATCHES]), [m])
            edge["read"] = [V("ext_copy", lambda e: e.tensor_copy(basei[:, :], bank[5][0:1, 0:BATCHES]), [m])]
            edge["dst_out"] = S.dma("scratch_out", dst_dram, dstT, [edge["copied"]])
            edge["wq_in"] = S.dma("wq_in", wq_s, w_qkv[:, 0:INNER].rearrange("(k p) c -> p k c", p=P), [edge["copied"]])

        def turn_wq(b):
            def make(e):
                for j in range(2 * b, 2 * b + 2):
                    for h in range(KH):
                        m = e.transpose(bank[5][:, (j % 2) * D + h * P:(j % 2) * D + (h + 1) * P],
                                        wq_s[:, h, j * P:(j + 1) * P], ident[:, :])
                return m
            m = T("turn_wq", make, [edge["wq_in"]] + edge["read"])
            edge["read"] = [V("wqT", lambda e: e.tensor_copy(
                wqT_a[:, 2 * b:2 * b + 2, :], bank[5][:, :].rearrange("p (j o) -> p j o", j=2)), [m])]
            if b:
                edge["wqT_out"] = S.dma("scratch_out", wqT_dram, wqT_a, edge["read"])

        order, closed, opened_to = [], [], 0

        def batches_to(n):
            for b in range(len(closed), min(n, BATCHES)):
                closed.append(START[opened_to] * P)
                order.append(("batch", b))

        def more(n=1):
            batches_to(len(closed) + n)

        def enough(g):
            return BATCHES if START[g + 1] == TILES else -(-START[g + 1] * P * E // N // BATCH) + LAG

        def ready(g, i):
            nonlocal opened_to
            if i == 0:
                batches_to(enough(g))
                opened_to = g + 1
                order.append(("mix", g, 0))
            elif i == 1:
                order.append(("mix_back", g, 0))
            elif i == 2:
                order.append(("mix", g, 1))
            elif i == 3:
                order.append(("mix_back", g, 1))
            elif i == 4:
                order.append(("norm", g))
            elif i == 6:
                order.append(("turn_norm", g, 0))
            elif i == 8 and SIZE[g] > 2:
                order.append(("turn_norm", g, 1))
            elif i == 9:
                order.append(("route", g))
            elif i == READY - 1:
                order.append(("turn_choice", g))

        READY = 12
        for t in range(TILES):
            order.append(("keys_values", t))
            if t:
                order.append(("dots", t - 1))
            if t in (2, 3):
                order.append(("zero_agg", t - 2))
            if t == 4:
                order.append(("general",))
            if t == 2 * GROUP:
                order.append(("load_experts",))
            if t >= AHEAD:
                more()
        order.append(("dots", TILES - 1))
        more()
        for i in range(3):
            order.append(("fold", i))
            more()
        for i in range(READY):
            ready(0, i)
            more()
        order += [("up", 0, 0), ("weigh", 0, 0)]
        first = len(closed)
        places = 2 * ((GROUPS - 2) * X + 1)
        place = 0

        def share():
            nonlocal place
            place += 1
            batches_to(first + min(place, places) * (BATCHES - first) // places)

        for g in range(GROUPS):
            for x_ in range(X):
                nxt = (g, x_ + 1) if x_ + 1 < X else (g + 1, 0)
                step = 2 * x_ - 2
                if nxt[0] < GROUPS:
                    order.append(("up", *nxt))
                if x_ == 0 and g:
                    order.append(("sum_back", g - 1, 0))
                if g + 1 < GROUPS and 0 <= step < READY:
                    ready(g + 1, step)
                share()
                if x_ == 0 and g:
                    order.append(("sum_back", g - 1, 1))
                if nxt[0] < GROUPS:
                    order.append(("weigh", *nxt))
                order.append(("down", g, x_))
                if g + 1 < GROUPS and 0 <= step + 1 < READY - 1:
                    ready(g + 1, step + 1)
                share()
                if g + 1 < GROUPS and step + 1 == READY - 1:
                    ready(g + 1, READY - 1)
            order.append(("sum_out", g))
        order += [("sum_back", GROUPS - 1, 0), ("sum_back", GROUPS - 1, 1)]
        assert len(closed) == BATCHES

        def even():
            b = 0
            while b < BATCHES:
                n = b
                while n < BATCHES and closed[n] == closed[b]:
                    n += 1
                r1 = V("bounds", lambda e, b=b, n=n: e.memset(rows[0:1, 2, b:n], float(closed[b])))
                b = n
            q = V("even", lambda e: e.tensor_tensor(rows[0:1, 3, :], rows[0:1, 0, :], rows[0:1, 2, :], ALU.is_ge), [edge["ext"], r1])
            q = V("even", lambda e: e.tensor_tensor(rows[0:1, 4, :], rows[0:1, 1, :], rows[0:1, 0, :], ALU.subtract), [edge["ext"]])
            q = V("even", lambda e: e.tensor_scalar(rows[0:1, 4, :], rows[0:1, 4, :], float(WINDOW), None, ALU.is_lt), [q])
            q = V("even", lambda e: e.tensor_tensor(rows[0:1, 5, :], rows[0:1, 3, :], rows[0:1, 4, :], ALU.mult), [q])
            q = V("even", lambda e: e.tensor_reduce(flag[:, 0:1], rows[0:1, 5, :], AX.X, ALU.min), [q])
            q = V("even", lambda e: e.tensor_scalar(flag[:, 1:2], flag[:, 0:1], -1.0, 1.0, ALU.mult, ALU.add), [q])
            edge["slow"] = V("even", lambda e: e.tensor_copy(slowi[:, :], flag[:, 1:2]), [q])

        def mask():
            m = T("slow_all", lambda e: e.matmul(bank[5][:, 0:1], ones1[:, :], flag[:, 1:2], start=True, stop=True),
                  [edge["slow"]] + edge["read"])
            q = V("mask", lambda e: e.tensor_scalar(slow_all[:, :], bank[5][:, 0:1], -float(2 * AGG), None, ALU.mult), [m])
            edge["read"] = [q]
            edge["offsets"] = V("mask", lambda e: e.tensor_scalar(offT[:, :, :], offT[:, :, :], slow_all[:, 0:1], None, ALU.add), [q])

        between = [lambda k=k: edge_rows(k) for k in range(2)]
        between += [lambda o=o, s=s, k=k: edge_turn(o, s, k)
                    for o, s in ((idxT, idx_f), (dstT, dst_f), (offT, off_f), (nrmT, nrm_f)) for k in range(2)]
        between += [edge_ext, even, mask, lambda: turn_wq(0), lambda: turn_wq(1)]
        assert len(between) <= 2 * FIRST_PIECE

        pieces = [(w, d, k, c) for w, d in ((w1, w1_dram), (w2, w2_dram)) for k in range(KH)
                  for c in range(X * D // BANK)]
        piece_in, piece_split, piece_out = {}, {}, {}
        PX = BANK // D

        def load_piece(n):
            w, _, k, c = pieces[n]
            piece_in[n] = S.dma(f"piece_in{n % 2}", piece_raw[:, n % 2, :].rearrange("p (x o) -> p x o", o=D),
                                w[c * PX:(c + 1) * PX, k * P:(k + 1) * P, :].rearrange("x p o -> p x o"),
                                [piece_split[n - 2]] if n >= 2 else [edge["copied"]])

        def split_piece(n):
            _, d, k, c = pieces[n]
            high, piece_split[n] = split("piece", lambda i: piece_p[:, n % 2, i, :], piece_raw[:, n % 2, :],
                                         [piece_in[n]] + ([piece_out[n - 2]] if n >= 2 else []))
            for i in range(2):
                piece_out[n] = S.dma(f"piece_out{n % 2}", d[:, i, k, c * BANK:(c + 1) * BANK],
                                     raw(piece_p[:, n % 2, i, :]), [high, piece_split[n]])

        for t in range(TILES):
            if t + 3 < TILES:
                load_x(t + 3)
            if t + 2 < TILES:
                ln_stats(t + 2)
                ln_sqrt(t + 2)
            if t:
                messages(t, 0)
            evacuate(t, 0)
            if t + 1 < TILES:
                turn(t + 1)
            if t:
                messages(t, 1)
            evacuate(t, 1)
            if t + 1 < TILES:
                copy_turned(t + 1)
            for n in range(2, 5):
                if t or n > 2:
                    messages(t, n)
                evacuate(t, n)
            if t + 1 < TILES:
                gates(t + 1)
            if t + 2 < TILES:
                normalize(t + 2)
            for n in range(5, NB):
                messages(t, n)
                evacuate(t, n)
                if n == 5 and between:
                    between.pop(0)()
            if between:
                between.pop(0)()
            if t + 1 < TILES:
                sigmoid(t + 1)
            p = t - FIRST_PIECE
            if 0 <= p <= len(pieces):
                if p:
                    split_piece(p - 1)
                for i in ((0, 1) if p == 0 else (p + 1,)):
                    if i < len(pieces):
                        load_piece(i)
            if t == FIRST_PIECE - 1:
                kv_split = center_kv()
            if t == START[1]:
                load_kv(0, [xnT_stored[t - 1], xnT_stored[t - 2], xnT_stored[t - 3]])
            store(t)
        table_in = [stored[TILES - 1], stored[TILES - 2]]
        phase_a = table_in + [table_read[TILES - 1], piece_out[len(pieces) - 1], piece_out[len(pieces) - 2],
                              edge["wqT_out"], edge["dst_out"], kv_split[1], xnT_stored[TILES - 1], xnT_stored[TILES - 2], xn_made[TILES - 1]]

        table_rows = table.rearrange("n (r o) -> (n r) o", r=R)
        g_free, g_idx, g_msg, g_oh, g_ps, g_add = (S.sem(f"general_{n}") for n in ("free", "idx", "msg", "onehot", "psum", "add"))
        from_pe, from_dve = bank[0], bank[0]

        def general_pool(e):
            slow = e.value_load(slowi[0:1, 0:1], min_val=0, max_val=1)
            with e.If(slow):
                with e.Fori(0, BATCHES) as b:
                    e.wait_ge(g_free, b + 1)
                    e.tensor_copy(idxG[:, :], idxT[:, :, bass.ds(b, 1)].rearrange("p j o -> p (j o)")).then_inc(g_idx, 1)
                    e.wait_ge(g_idx, b + 1)
                    e.tensor_tensor(carrier[:, :], carrier[:, :], carrier[:, :], ALU.add)
                    for j in range(CHUNKS):
                        e.indirect_dma_start(msg[:, 0, j, :], None, table_rows,
                                             bass.IndirectOffsetOnAxis(idxG[:, j:j + 1], 0)).then_inc(g_msg, 16)
                    e.wait_ge(g_msg, b * 16 * CHUNKS + 16 * CHUNKS)
                e.wait_ge(g_free, BATCHES + 1)

        def general_vector(e):
            slow = e.value_load(slowi[0:1, 0:1], min_val=0, max_val=1)
            with e.If(slow):
                e.sem_inc(g_free, 1)
                with e.Fori(0, BATCHES) as b:
                    e.tensor_copy(dstG.unsqueeze(2), dstL[:, :, bass.ds(b, 1)])
                    e.tensor_copy(nrmG.unsqueeze(2), nrmT[:, :, bass.ds(b, 1)]).then_inc(g_add, 1)
                    with e.Fori(0, TILES) as w:
                        e.wait_ge(g_add, b * (2 * TILES + 1) + 1)
                        for j in range(CHUNKS):
                            o = e.tensor_scalar(onehot[:, 0, j, :], iota[:, :], dstG[:, j:j + 1], nrmG[:, j:j + 1],
                                                ALU.is_equal, ALU.mult)
                        o.then_inc(g_oh, 1)
                        e.wait_ge(g_ps, b * TILES + w + 1)
                        e.tensor_scalar(dstG, dstG, float(P), None, ALU.subtract).then_inc(g_add, 1)
                        cols = agg[:, :, bass.ds(w * P, P)]
                        e.tensor_tensor(cols, cols, from_pe[:, 0:D].rearrange("p (h n) -> p h n", h=KH),
                                        ALU.add).then_inc(g_add, 1)
                        e.wait_ge(g_add, b * (2 * TILES + 1) + w * 2 + 3)
                    e.sem_inc(g_free, 1)

        def general_tensor(e):
            slow = e.value_load(slowi[0:1, 0:1], min_val=0, max_val=1)
            with e.If(slow):
                with e.Fori(0, BATCHES) as b:
                    with e.Fori(0, TILES) as w:
                        e.wait_ge(g_msg, b * 16 * CHUNKS + 16 * CHUNKS)
                        e.wait_ge(g_oh, b * TILES + w + 1)
                        for h in range(KH):
                            for j in range(CHUNKS):
                                m = e.matmul(from_dve[:, h * P:(h + 1) * P], msg[:, 0, j, h * P:(h + 1) * P],
                                             onehot[:, 0, j, :], start=j == 0, stop=j == CHUNKS - 1)
                        m.then_inc(g_ps, 1)

        agg_zero = []

        def zero_agg(i):
            half = slice(i * AGG // 2, (i + 1) * AGG // 2)
            agg_zero.append(V("agg_zero", lambda e: e.memset(agg[:, 0, half], 0.0), phase_a))
            agg_zero.append(A("agg_zero_act", lambda e: e.memzero(agg[:, 1, half]), phase_a))

        def general():
            slow, idx_made = edge["slow"], edge["offsets"]
            S.put("gpsimd", None, general_pool, table_in + [slow, idx_made])
            S.put("vector", None, general_vector, phase_a + agg_zero + [slow, dst_back])
            S.put("tensor", None, general_tensor, phase_a + [slow])

        gathered, hot, summed, added, base = {}, {}, {}, {}, {}

        def gather(b):
            after = [summed[b - SLOTS]] if b >= SLOTS else phase_a + [edge["offsets"]] + [dst_back] * (b == SLOTS - 1)
            def make(e):
                for j in range(CHUNKS):
                    m = e.indirect_dma_start(msg[:, b % SLOTS, j, :], None, table_rows,
                                             bass.IndirectOffsetOnAxis(idxT[:, j, b:b + 1], 0))
                    if j < CHUNKS - 1:
                        m.then_inc(S.sem(f"gather{b % SLOTS}"), 16)
                return m
            S.put("gpsimd", f"gather{b % SLOTS}", make, after, by=16)
            S.value[f"gather{b % SLOTS}"] += 16 * (CHUNKS - 1)
            gathered[b] = (f"gather{b % SLOTS}", S.value[f"gather{b % SLOTS}"])

        def one_hot(b):
            def make(e):
                for j in range(CHUNKS):
                    m = e.tensor_scalar(onehot[:, b % HOTS, j, :], iota[:, :], offT[:, j, b:b + 1], nrmT[:, j, b:b + 1],
                                        ALU.is_equal, ALU.mult)
                return m
            hot[b] = V("onehot", make, ([summed[b - HOTS]] if b >= HOTS else phase_a + [edge["offsets"]]))

        def sum_batch(b):
            ps = bank[b % 2]
            def make(e):
                for h in range(KH):
                    for j in range(CHUNKS):
                        m = e.matmul(ps[:, h * P:(h + 1) * P], msg[:, b % SLOTS, j, h * P:(h + 1) * P],
                                     onehot[:, b % HOTS, j, :], start=j == 0, stop=j == CHUNKS - 1)
                return m
            summed[b] = T("sum_batch", make, [gathered[b], hot[b]] + ([added[b - 2]] if b >= 2 else phase_a))

        def add_batch(b):
            def make(e):
                if b % BASES == 0:
                    n = min(BASES, BATCHES - b)
                    _, values = nc.values_load_multi_w_load_instructions(
                        basei[0:1, b:b + n], engines=[e.engine], min_val=0, max_val=AGG - WINDOW,
                        skip_runtime_bounds_check_because="a destination is a node")
                    base.update({b + i: v for i, v in enumerate(values)})
                cols = agg[:, :, bass.ds(base[b], WINDOW)]
                return e.tensor_tensor(cols, cols, bank[b % 2][:, 0:D].rearrange("p (h n) -> p h n", h=KH), ALU.add)
            added[b] = V("add_batch", make, [summed[b]] + ([added[b - 1]] + agg_read[-1:] if b else agg_zero))

        def batch(b):
            if b == 0:
                for i in range(min(SLOTS, BATCHES)):
                    gather(i)
                for i in range(HOTS - 1):
                    one_hot(i)
            if b + HOTS - 1 < BATCHES:
                one_hot(b + HOTS - 1)
            sum_batch(b)
            if b + SLOTS < BATCHES:
                gather(b + SLOTS)
            add_batch(b)
            added_last[0] = added[b]

        added_last, agg_read = [None], []
        
        dots_done, kv_read = {}, {}
        squared, v_made, k_made, roots, reduced = {}, {}, {}, {}, {}
        HEADS = INNER // HEAD

        def keys_values(t):
            g, k = PLACE[t]
            if k == 0 and 1 <= g < GROUPS - 1:
                load_kv(g + 1, [kv_done[t - 1]])
            banks = (3, 4) if t % 2 == 0 else (6, 7)
            def make(e):
                for c in range(VK // BANK):
                    for h in range(KH):
                        m = three(e, bank[banks[c]][:, :], lambda q: xnT_kv[:, (g + 1) % 2, q, h, k * P:(k + 1) * P],
                                  lambda q: wkv_p[:, q, h, c * BANK:(c + 1) * BANK], h == 0, h == KH - 1)
                return m
            kv_done[t] = T("keys_values", make, [kv_in[g], kv_split[1]] + (kv_read[t - 2] if t >= 2 else evacuated[-MB:] + [gate_made[TILES - 1], xnT_made[TILES - 1]]))
            free = [reduced[t - 1]] if t else [xn_made[TILES - 1], turned[TILES - 1], kv_split[1], edge["slow"]]
            for c in range(2):
                squared[t] = A("squares", lambda e, c=c: e.activation(
                    sq[:, c * INNER:(c + 1) * INNER], bank[banks[c]][:, :], ACT.Square), [kv_done[t]] + free)
            v_made[t] = A("values", lambda e: e.copy(v_s[:, t % 2, :], bank[banks[1]][:, :]),
                          [dots_done[t - 2]] if t >= 2 else [])
            s = reduced[t] = V("head_vars", lambda e: e.tensor_reduce(
                hs[:, 0, :], sq.rearrange("p (h d) -> p h d", d=HEAD), AX.X, ALU.add), [squared[t]])
            s = V("head_vars", lambda e: e.tensor_scalar(hs[:, 1, :], hs[:, 0, :], 1.0 / HEAD, EPS, ALU.mult, ALU.add), [s])
            s = V("head_vars", lambda e: e.tensor_tensor(
                hs[:, 2, 0:HEADS], hs[:, 1, 0:HEADS], hs[:, 1, HEADS:2 * HEADS], ALU.mult), [s])
            s = A("head_sqrt", lambda e: e.activation(hs[:, 3, 0:HEADS], hs[:, 2, 0:HEADS], ACT.Sqrt), [s])
            s = V("keys", lambda e: e.reciprocal(hs[:, 4, 0:HEADS], hs[:, 3, 0:HEADS]), [s])
            k_made[t] = V("keys", lambda e: e.tensor_tensor(
                k_s[:, t % 2, :].rearrange("p (h d) -> p h d", d=HEAD),
                bank[banks[0]][:, :].rearrange("p (h d) -> p h d", d=HEAD),
                hs[:, 4, 0:HEADS].unsqueeze(2).to_broadcast([P, HEADS, HEAD]), ALU.mult),
                [s] + ([dots_done[t - 2]] if t >= 2 else []))
            kv_read[t] = [squared[t], v_made[t], k_made[t]]

        def dots(t):
            def make(e):
                for j in range(PAIRS):
                    m = e.matmul(bank[5][:, j * P:(j + 1) * P], v_s[:, t % 2, j * P:(j + 1) * P],
                                 k_s[:, t % 2, j * P:(j + 1) * P],
                                 start=t == 0 and j == 0, stop=t == TILES - 1, skip_group_check=True)
                return m
            dots_done[t] = T("dots", make, [v_made[t], k_made[t]] + (edge["read"] if t == 0 else []))

        folded = {}

        def fold_step(i):
            if i == 0:
                folded["in"] = S.dma("fold_w", wqT, wqT_dram, [reduced[TILES - 1], edge["wqT_out"]])
                z = V("fold_zero", lambda e: e.memset(bd, 0.0), [dots_done[TILES - 1]])
                for q in range(2):
                    half = slice(q * HEAD, (q + 1) * HEAD)
                    folded["bd"] = V("fold_dots", lambda e, half=half: e.tensor_scalar(
                        bd[half, :, half], bank[5][half, :].rearrange("p (j d) -> p j d", j=PAIRS)[:, :, half],
                        1.0 / N, None, ALU.mult), [z])
            elif i == 1:
                def fold_out(e):
                    for j in range(PAIRS):
                        m = e.matmul(bank[3 + j // 2][:, (j % 2) * D:(j % 2 + 1) * D], bd[:, j, :], wout_s[:, j, :],
                                     start=True, stop=True)
                    return m
                m = T("fold_out", fold_out, [folded["bd"], wout_in] + kv_read[TILES - 1])
                for b in range(2):
                    folded["out"] = V("fold_copy", lambda e, b=b: e.tensor_copy(
                        fold[:, 2 * b:2 * b + 2, :], bank[3 + b][:, :].rearrange("p (j o) -> p j o", j=2)), [m])
            else:
                def fold_in(e):
                    for h in range(KH):
                        for j in range(PAIRS):
                            m = e.matmul(bank[2][:, h * D:(h + 1) * D], wqT[:, j, h * P:(h + 1) * P], fold[:, j, :],
                                         start=j == 0, stop=j == PAIRS - 1)
                    return m
                m = T("fold_in", fold_in, [folded["out"], folded["in"]])
                folded["mix"] = split("mix", lambda q: mix_p[:, q, :, :],
                                      bank[2][:, :].rearrange("p (h o) -> p h o", h=KH), [m])
                fold_done.append(folded["mix"][1])
                load_group(0, fold_done)
                load_group(1, fold_done)

        experts_in, fold_done, turned_comb, combT_made = [], [], {}, {}
        group_in, xnT_in, x2_made, acc_made = {}, {}, {}, {}
        x3_made, x3T_made, comb_made, store_out = {}, {}, {}, {}
        misc_read, turn_read, xT_read = [], [], []
        x3_turned, up_last, rstd = [], {}, {}

        def load_group(g, after=()):
            K = SIZE[g]
            after = list(after) + ([store_out[g - 2]] if g >= 2 else [])
            full = K if (START[g] + K) * P <= N else K - 1
            n0 = START[g] * P
            if full:
                group_in[g] = S.dma(f"group_x{g % 2}", acc[:, g % 2, 0:full, :],
                                    x[n0:n0 + full * P, :].rearrange("(k p) o -> p k o", p=P), after)
            if full < K:
                group_in[g] = S.dma(f"group_x{g % 2}", acc[0:LAST, g % 2, full, :], x[n0 + full * P:N, :], after)

        def load_group_xnT(g, after=()):
            K = SIZE[g]
            xnT_in[g] = S.dma("group_xnT", raw(xnT_g)[:, :, :, 0:K * P], xnT_dram[g, :, :, :, 0:K * P], after)

        def turn_back(g, h):
            s, K = g % 2, SIZE[g]
            def make(e):
                for k in range(K):
                    m = e.transpose(bank[3][:, k * P:(k + 1) * P], xT[:, k * P:(k + 1) * P], ident[:, :])
                return m
            m = T("turn_back", make, xT_read[-1:] + misc_read[-1:])
            xT_read.append(m)
            misc_read.append(V("acc_add", lambda e: e.tensor_tensor(
                acc[:, s, 0:K, h * P:(h + 1) * P], acc[:, s, 0:K, h * P:(h + 1) * P],
                bank[3][:, 0:K * P].rearrange("p (k o) -> p k o", k=K), ALU.add),
                [m, group_in[g]]))
            return misc_read[-1]

        def mix(g, h):
            s, n0, n = g % 2, START[g] * P, SIZE[g] * P
            def make(e):
                for q in range(KH):
                    m = three(e, bank[3][:, 0:n], lambda i: mix_p[:, i, q, h * P:(h + 1) * P],
                              lambda i: xnT_g[:, i, q, 0:n], q == 0, q == KH - 1)
                return m
            m = T("mix_sum", make, [xnT_in[g], folded["mix"][1]] + misc_read[-1:])
            c = A("mix_copy", lambda e: e.activation(xT[:, 0:n], bank[3][:, 0:n], ACT.Identity,
                                                     bias=boutT[:, h:h + 1]), [m] + xT_read[-1:] + fold_done)
            misc_read.append(c)
            xT_read.append(V("relu_add", lambda e: e.scalar_tensor_tensor(
                xT[:, 0:n], agg[:, h, n0:n0 + n], 0.0, xT[:, 0:n], ALU.max, ALU.add), [c, added_last[0]]))
            agg_read.append(xT_read[-1])
            if h == KH - 1 and g + 1 < GROUPS:
                load_group_xnT(g + 1, [m])

        def mix_back(g, h):
            s, K = g % 2, SIZE[g]
            a = turn_back(g, h)
            if h < KH - 1:
                return
            for k in range(K):
                q = V("x2_stats", lambda e, k=k: e.bn_stats(stB[:, k, 0:6], acc[:, s, k, :]), [a])
            for k in range(K):
                q1 = V("x2_stats", lambda e, k=k: e.bn_aggr(mvB[:, k, :], stB[:, k, 0:6]), [q])
            x2_made[g] = V("x2_stats", lambda e: e.tensor_scalar(
                sdB[:, 0, 0:K].unsqueeze(2), mvB[:, 0:K, 1:2], EPS, None, ALU.add), [q1])

        def norm_group(g):
            K = SIZE[g]
            q = A("x2_sqrt", lambda e: e.activation(sdB[:, 1, 0:K], sdB[:, 0, 0:K], ACT.Sqrt), [x2_made[g]])
            rstd[g] = V("x2_rstd", lambda e: e.reciprocal(sdB[:, 2, 0:K], sdB[:, 1, 0:K]), [q])
            for k in range(min(2, K)):
                norm_tile(g, k)

        def norm_tile(g, k):
            s = g % 2
            x3_made[g, k] = V("x3", lambda e: e.tensor_scalar(
                x3[:, k % 2, :], acc[:, s, k, :], mvB[:, k, 0:1], sdB[:, 2, k:k + 1], ALU.subtract, ALU.mult),
                [rstd[g]] + (x3_turned[-2:] or fold_done))

        def turn_norm(g, i):
            s, ks = g % 2, range(2 * i, min(2 * i + 2, SIZE[g]))
            def make(e):
                for k in ks:
                    for h in range(KH):
                        m = e.transpose(bank[3][:, h * 2 * P + (k % 2) * P:h * 2 * P + (k % 2 + 1) * P],
                                        x3[:, k % 2, h * P:(h + 1) * P], ident[:, :])
                return m
            m = T("turn_x3", make, [x3_made[g, ks[-1]]] + misc_read[-1:])
            n0, n = 2 * i * P, len(ks) * P
            high, x3T_made[g] = split("x3T", lambda q: x3T[:, s, q, :, n0:n0 + n],
                                      bank[3][:, :].rearrange("p (h n) -> p h n", h=KH)[:, :, 0:n],
                                      [m] + ([up_last[g - 2]] if g >= 2 else []))
            misc_read.append(x3T_made[g])
            for k in ks:
                q = acc_made[g] = V("acc", lambda e, k=k: e.tensor_tensor(
                    acc[:, s, k, :], acc[:, s, k, :], x3[:, k % 2, :], ALU.add), [x3_made[g, k]])
            x3_turned.extend([m, q])
            if i == 0:
                for k in range(2, SIZE[g]):
                    norm_tile(g, k)

        def route_group(g):
            s, K = g % 2, SIZE[g]
            def make(e):
                for k in range(K):
                    for h in range(KH):
                        for i in range(2):
                            m = e.matmul(bank[3][:, k * 2 * X:(k + 1) * 2 * X], x3T[:, s, i, h, k * P:(k + 1) * P],
                                         route_p[:, h, :, :].rearrange("p i x -> p (i x)"),
                                         start=h == i == 0, stop=h == KH - 1 and i == 1)
                return m
            m = T("logits", make, [x3T_made[g], route_split])
            sides = bank[3][:, 0:K * 2 * X].rearrange("p (k i x) -> p k i x", i=2, x=X)
            lg = lgB[:, 0, 0:K, :]
            q = V("softmax", lambda e: e.tensor_copy(lg, sides[:, :, 1, :]), [m])
            m = V("softmax", lambda e: e.tensor_tensor(lg, lg, sides[:, :, 0, :], ALU.add), [q])
            misc_read.append(m)
            wide = lambda v: v.unsqueeze(2).to_broadcast([P, K, X])
            q = V("softmax", lambda e: e.tensor_reduce(smB[:, 0, 0:K], lg, AX.X, ALU.max), [m])
            q = V("softmax", lambda e: e.tensor_tensor(lgB[:, 0, 0:K, :], lg, wide(smB[:, 0, 0:K]), ALU.subtract), [q])
            q = A("exp", lambda e: e.activation(lgB[:, 1, 0:K, :], lgB[:, 0, 0:K, :], ACT.Exp), [q])
            q = V("softmax", lambda e: e.tensor_reduce(smB[:, 1, 0:K], lgB[:, 1, 0:K, :], AX.X, ALU.add), [q])
            q = V("softmax", lambda e: e.reciprocal(smB[:, 2, 0:K], smB[:, 1, 0:K]), [q])
            comb_made[g] = V("softmax", lambda e: e.tensor_tensor(
                lgB[:, 2, 0:K, :], lgB[:, 1, 0:K, :], wide(smB[:, 2, 0:K]), ALU.mult), [q])
            choose_group(g)

        def choose_group(g):
            s, K = g % 2, SIZE[g]
            q = comb_made[g]
            for k in range(K):
                q1 = V("top2", lambda e, k=k: e.max(topB[:, k, :], lgB[:, 2, k, :]), [q])
            for k in range(K):
                q2 = V("top2", lambda e, k=k: e.max_index(topi[:, k, :], topB[:, k, :], lgB[:, 2, k, :]), [q1])
            q = V("top2", lambda e: e.tensor_tensor(smB[:, 3, 0:K].unsqueeze(2), topB[:, 0:K, 0:1], topB[:, 0:K, 1:2], ALU.add), [q1])
            q = V("top2", lambda e: e.tensor_scalar(smB[:, 4, 0:K], smB[:, 3, 0:K], 1e-12, None, ALU.max), [q])
            q = V("top2", lambda e: e.reciprocal(smB[:, 5, 0:K], smB[:, 4, 0:K]), [q])
            V("top2", lambda e: e.tensor_copy(wB[:, 1, 0:K, :], topi[:, 0:K, 0:2]), [q2])
            q = V("top2", lambda e: e.tensor_tensor(wB[:, 0, 0:K, :], topB[:, 0:K, 0:2],
                                                    smB[:, 5, 0:K].unsqueeze(2).to_broadcast([P, K, 2]), ALU.mult), [q])
            for k in range(K):
                for i in range(2):
                    q1 = V("top2", lambda e, k=k, i=i: e.tensor_scalar(
                        combB[:, i, k, :], iota[:, 0:X], wB[:, 1, k, i:i + 1], wB[:, 0, k, i:i + 1], ALU.is_equal, ALU.mult),
                        [q])
            q = V("top2", lambda e: e.tensor_tensor(combB[:, 0, 0:K, :], combB[:, 0, 0:K, :], combB[:, 1, 0:K, :], ALU.add), [q1])
            q = V("top2", lambda e: e.tensor_copy(comb_p[:, 0:K, 0, :], combB[:, 0, 0:K, :]),
                  [q] + ([turned_comb[g - 1]] if g else []))
            comb_made[g] = V("top2", lambda e: e.tensor_tensor(
                comb_p[:, 0:K, 1, :], combB[:, 0, 0:K, :], raw(comb_p)[:, 0:K, 0, :], ALU.subtract), [q])

        def turn_choice(g):
            K = SIZE[g]
            def make(e):
                for k in range(K):
                    m = e.transpose(bank[3][0:2 * X, k * P:(k + 1) * P], raw(comb_p)[:, k, :, :].rearrange("p i x -> p (i x)"),
                                    ident[:, :])
                return m
            m = turned_comb[g] = T("turn_comb", make, [comb_made[g]] + misc_read[-1:])
            combT_made[g] = A("combT", lambda e: e.copy(combT[0:2 * X, 0:K * P], bank[3][0:2 * X, 0:K * P]),
                              [m] + ([comb_used[g - 1]] if g else []))
            misc_read.append(combT_made[g])

        comb_used, y_read, gelus = {}, {}, {}
        low_made, down_order, up_read = [], [], []

        def up(g, x_):
            s, n = g % 2, SIZE[g] * P
            gelus[g, x_] = []
            for f in range(KH):
                def make(e, f=f):
                    for h in range(KH):
                        m = three(e, bank[4 + f][:, 0:n], lambda i: w1_p[:, i, h, x_, f * P:(f + 1) * P],
                                  lambda i: x3T[:, s, i, h, 0:n], h == 0, h == KH - 1)
                    return m
                m = up_last[g] = T("up", make, [x3T_made[g], experts_in[-1]] + ([up_read[-2]] if len(up_read) >= 2 else []))
                up_read.append(A("gelu", lambda e, f=f: e.activation(
                    g_s[:, f, 0:n], bank[4 + f][:, 0:n], ACT.Gelu, bias=b1T[:, x_ * KH + f:x_ * KH + f + 1]),
                    [m] + (low_made[-1:] or fold_done)))
                gelus[g, x_].append(up_read[-1])

        def weigh(g, x_):
            n, slot = SIZE[g] * P, (g * X + x_) % 2
            sp = comb_used[g] = T("spread", lambda e: e.matmul(
                bank[2][:, 0:n], pick[0:2 * X, x_:x_ + 1].to_broadcast([2 * X, P]), combT[0:2 * X, 0:n],
                start=True, stop=True), [combT_made[g], pick_made] + turn_read[-1:])
            for f in range(KH):
                w = V("weight", lambda e, f=f: e.tensor_tensor(g_s[:, f, 0:n], g_s[:, f, 0:n], bank[2][:, 0:n], ALU.mult),
                      [sp, gelus[g, x_][f]])
                high, low = split("h", lambda i, f=f: h_p[:, slot, i, f, 0:n], g_s[:, f, 0:n], [w] + down_order[-1:])
            turn_read.append(w)
            low_made.append(low)

        def down(g, x_):
            n, e_i = SIZE[g] * P, g * X + x_
            def make(e):
                for o in range(KH):
                    y = bank[6 + o][:, 0:n]
                    if x_ == 0:
                        for i in range(2):
                            e.matmul(y, b2_p[0:2 * X, i, o * P:(o + 1) * P], combT[0:2 * X, 0:n], start=i == 0, stop=False)
                    for f in range(KH):
                        m = three(e, y, lambda i: w2_p[:, i, f, x_, o * P:(o + 1) * P],
                                  lambda i: h_p[:, e_i % 2, i, f, 0:n], False, x_ == X - 1 and f == KH - 1)
                return m
            m = T("down", make, [low_made[e_i], b2_made] + ([y_read[g - 1]] if g and x_ == 0 else []))
            comb_used[g] = m
            down_order.append(m)

        def sum_out(g, h=0):
            n = SIZE[g] * P
            c = y_read[g] = A("y_copy", lambda e: e.copy(xT[:, 0:n], bank[6 + h][:, 0:n]), [down_order[-1]] + xT_read[-1:])
            xT_read.append(c)

        def sum_back(g, h):
            s, K = g % 2, SIZE[g]
            a = turn_back(g, h)
            if h < KH - 1:
                sum_out(g, h + 1)
                return
            full = K if (START[g] + K) * P <= N else K - 1
            n0 = START[g] * P
            if full:
                store_out[g] = S.dma(f"out_store{s}", out[n0:n0 + full * P, :].rearrange("(k p) o -> p k o", p=P),
                                     acc[:, s, 0:full, :], [a, acc_made[g]])
            if full < K:
                store_out[g] = S.dma(f"out_store{s}", out[n0 + full * P:N, :], acc[0:LAST, s, full, :], [a, acc_made[g]])
            if g + 2 < GROUPS:
                load_group(g + 2)

        load_kv(1, phase_a)
        dst_back = S.dma("dst_in", dstL, dst_dram, phase_a)
        wout_in = S.dma("wout_in", wout_s, w_out.rearrange("(j p) o -> p j o", p=P), phase_a)

        def load_experts():
            load_group_xnT(0, phase_a)
            for o, d in ((w1_p, w1_dram), (w2_p, w2_dram)):
                for q in range(2):
                    experts_in.append(S.dma("experts_in", raw(o[:, q, :, :, :]).rearrange("p k x o -> p k (x o)"),
                                            d[:, q, :, :], phase_a))

        steps = {"batch": batch, "mix": mix, "mix_back": mix_back, "norm": norm_group, "turn_norm": turn_norm,
                 "route": route_group, "turn_choice": turn_choice, "up": up, "weigh": weigh, "down": down,
                 "sum_out": sum_out, "sum_back": sum_back,
                 "keys_values": keys_values, "dots": dots, "fold": fold_step, "zero_agg": zero_agg,
                 "general": general, "load_experts": load_experts}
        for name, *args in order:
            steps[name](*args)
        finals = {s: v for s, v in S.value.items() if s.startswith(("out_store", "table_store", "xnT_store", "piece_out", "scratch_out"))}

        block = ctx.enter_context(nc.Block())

        @block.sync
        def _(eng):
            for emit in S.queue["sync"]:
                emit(eng)
            for name, value in finals.items():
                eng.wait_ge(S.sem(name), value)

        @block.scalar
        def _(eng):
            for emit in S.queue["scalar"]:
                emit(eng)

        @block.vector
        def _(eng):
            for emit in S.queue["vector"]:
                emit(eng)

        @block.gpsimd
        def _(eng):
            for emit in S.queue["gpsimd"]:
                emit(eng)

        @block.tensor
        def _(eng):
            for emit in S.queue["tensor"]:
                emit(eng)


_INS = ["x", "src", "dst", "edge_type_16", "edge_weight1", "L0_gnn_weight", "L0_gnn_gate_weight", "L0_mix_w_qkv",
        "L0_mix_w_out", "L0_mix_b_out", "L0_ffn_router_w", "L0_ffn_w1", "L0_ffn_b1", "L0_ffn_w2", "L0_ffn_b2"]


def kernel(**inputs):
    import numpy as np
    import concourse.bacc as bacc
    from concourse.bass_utils import run_bass_kernel_spmd as run

    nc = bacc.Bacc("TRN2", target_bir_lowering=False, num_devices=1, dynamic_dma_scratch_size=8192)
    arrays, args = {}, []
    for name in _INS:
        a = np.ascontiguousarray(inputs[name])
        arrays[f"in_{name}"] = a
        args.append(nc.dram_tensor(f"in_{name}", a.shape, mybir.dt.from_np(a.dtype), kind="ExternalInput").ap())
    shape = arrays["in_x"].shape
    args.append(nc.dram_tensor("out_dram", shape, F32, kind="ExternalOutput").ap())
    gps_layer(nc, *args)
    r = run(nc, [arrays], core_ids=[0])
    return r.results[0]["out_dram"]
```
